# Optimizing a Trainium2 kernel written in Bass

```python
import numpy as np
import jax
import jax.numpy as jnp

def _softmax(x, axis=-1):
    return jax.nn.softmax(x, axis=axis)

def _gelu(x):
    return jax.nn.gelu(x, approximate=True)

def _silu(x):
    return jax.nn.silu(x)

def _sigmoid(x):
    return jax.nn.sigmoid(x)

def _layernorm(x, axis=-1, eps=1e-05):
    m = jnp.mean(x, axis=axis, keepdims=True)
    v = jnp.var(x, axis=axis, keepdims=True)
    return (x - m) / jnp.sqrt(v + eps)

def _scatter_add(tgt, idx, src, axis=0):
    return tgt.at[idx].add(src)

def _segment_sum(src, seg, n):
    return jax.ops.segment_sum(src, seg, n)
kernel_name = 'mk_decoder_preln_d2_seqx_r8_9af73f'

def setup_inputs(seed: int=0):
    np.random.seed(seed)
    _w = jnp.asarray

    def _rec_inputs():
        import jax
        import jax.numpy as jnp
        _rk = jax.random.key(seed)
        x = 7.22e-05 + 1 * jax.random.normal(jax.random.fold_in(_rk, 1), (64, 64, 128), jnp.float32)
        _lenS = 64 - jax.random.randint(jax.random.fold_in(_rk, 7), (64,), 0, max(1, 64 // 4) + 1, jnp.int32)
        _lenS2 = 64 - jax.random.randint(jax.random.fold_in(_rk, 8), (64,), 0, max(1, 64 // 4) + 1, jnp.int32)
        _ctx_768P = jax.random.normal(jax.random.fold_in(_rk, 11), (64, 16, 96), jnp.float32)
        _ctx_768c = jax.random.dirichlet(jax.random.fold_in(_rk, 511), 0.3 * jnp.ones((16,), jnp.float32), (64, 64))
        _ctx_768t = jnp.einsum('bsk,bkd->bsd', _ctx_768c, _ctx_768P)
        _ctx_768t = _ctx_768t * jax.lax.rsqrt(jnp.mean(jnp.square(_ctx_768t)) + 1e-12) * 0.953939
        ctx_768 = -0.000191848 + 0.999787 * (_ctx_768t + 0.3 * jax.random.normal(jax.random.fold_in(_rk, 611), (64, 64, 96), jnp.float32))
        return (x, ctx_768)
    x, ctx_768 = _rec_inputs()

    def _L0_attn_setup():
        import math
        import jax, jax.numpy as jnp
        import numpy as np
        D_MODEL = 128
        D_STATE = 16
        D_CONV = 4
        EXPAND = 2
        D_INNER = EXPAND * D_MODEL
        DT_RANK = math.ceil(D_MODEL / 16)
        BATCH, SEQ = (1, 256)
        DT_MIN, DT_MAX, DT_FLOOR = (0.001, 0.1, 0.0001)

        def _mamba(x, W_in, conv_w, conv_b, W_x, W_dt, b_dt, A_log, D, W_out):
            B, L, _ = x.shape
            xz = x @ W_in.T
            xs, z = jnp.split(xz, 2, axis=-1)
            xc = jnp.pad(xs.transpose(0, 2, 1), ((0, 0), (0, 0), (D_CONV - 1, 0)))
            xc = jax.lax.conv_general_dilated(xc, conv_w, (1,), 'VALID', dimension_numbers=('NCH', 'OIH', 'NCH'), feature_group_count=D_INNER)
            xs = jax.nn.silu(xc.transpose(0, 2, 1) + conv_b[None, None, :])
            A = -jnp.exp(A_log)
            x_dbl = xs @ W_x.T
            dt, Bm, Cm = jnp.split(x_dbl, [DT_RANK, DT_RANK + D_STATE], axis=-1)
            dt = jax.nn.softplus(dt @ W_dt.T + b_dt)
            dA = jnp.exp(dt[..., None] * A)
            dBx = dt[..., None] * Bm[:, :, None, :] * xs[..., None]

            def step(h, inputs):
                dA_t, dBx_t, C_t = inputs
                h = dA_t * h + dBx_t
                y = jnp.einsum('bdn,bn->bd', h, C_t)
                return (h, y)
            h0 = jnp.zeros((B, D_INNER, D_STATE), xs.dtype)
            _, ys = jax.lax.scan(step, h0, (dA.transpose(1, 0, 2, 3), dBx.transpose(1, 0, 2, 3), Cm.transpose(1, 0, 2)))
            y = ys.transpose(1, 0, 2) + xs * D
            return y * jax.nn.silu(z) @ W_out.T
        key = jax.random.key(seed)
        ks = jax.random.split(key, 8)
        x = jax.random.normal(ks[0], (BATCH, SEQ, D_MODEL), jnp.float32)
        W_in = jax.random.normal(ks[1], (2 * D_INNER, D_MODEL), jnp.float32) / np.sqrt(D_MODEL)
        conv_w = jax.random.normal(ks[2], (D_INNER, 1, D_CONV), jnp.float32) / np.sqrt(D_CONV)
        conv_b = jnp.zeros((D_INNER,), jnp.float32)
        W_x = jax.random.normal(ks[3], (DT_RANK + 2 * D_STATE, D_INNER), jnp.float32) / np.sqrt(D_INNER)
        dt_std = DT_RANK ** (-0.5)
        W_dt = jax.random.uniform(ks[4], (D_INNER, DT_RANK), jnp.float32, -dt_std, dt_std)
        dt = jnp.exp(jax.random.uniform(ks[5], (D_INNER,), jnp.float32) * (math.log(DT_MAX) - math.log(DT_MIN)) + math.log(DT_MIN))
        dt = jnp.clip(dt, DT_FLOOR, None)
        b_dt = dt + jnp.log(-jnp.expm1(-dt))
        A_log = jnp.log(jnp.tile(jnp.arange(1, D_STATE + 1, dtype=jnp.float32), (D_INNER, 1)))
        D = jnp.ones((D_INNER,), jnp.float32)
        W_out = jax.random.normal(ks[6], (D_MODEL, D_INNER), jnp.float32) / np.sqrt(D_INNER)
        return {'x': x, 'W_in': W_in, 'conv_w': conv_w, 'conv_b': conv_b, 'W_x': W_x, 'W_dt': W_dt, 'b_dt': b_dt, 'A_log': A_log, 'D': D, 'W_out': W_out}
    _L0_attn_all = _L0_attn_setup()
    _L0_attn_in = {k: v for k, v in _L0_attn_all.items() if k in ('W_in', 'conv_w', 'conv_b', 'W_x', 'W_dt', 'b_dt', 'A_log', 'D', 'W_out')}
    del _L0_attn_all

    def _L0_xattn_setup():
        import jax, jax.numpy as jnp
        import numpy as np
        NUM_HEADS = 16
        CLAMP = 10000.0
        key = jax.random.key(seed)
        ks = jax.random.split(key, 8)
        B, Nq, Nkv, Cq, Ckv = (4, 256, 256, 128, 96)
        s_q = 1.0 / np.sqrt(Cq)
        s_kv = 1.0 / np.sqrt(Ckv)
        return {'query': jax.random.normal(ks[0], (B, Nq, Cq), jnp.float32), 'key_value': jax.random.normal(ks[1], (B, Nkv, Ckv), jnp.float32), 'Wq': jax.random.normal(ks[2], (Cq, Cq), jnp.float32) * s_q, 'bq': jnp.zeros((Cq,), jnp.float32), 'Wk': jax.random.normal(ks[3], (Ckv, Cq), jnp.float32) * s_kv, 'bk': jnp.zeros((Cq,), jnp.float32), 'Wv': jax.random.normal(ks[4], (Ckv, Cq), jnp.float32) * s_kv, 'bv': jnp.zeros((Cq,), jnp.float32), 'Wo': jax.random.normal(ks[5], (Cq, Cq), jnp.float32) * s_q, 'bo': jnp.zeros((Cq,), jnp.float32)}
    _L0_xattn_all = _L0_xattn_setup()
    _L0_xattn_in = {k: v for k, v in _L0_xattn_all.items() if k in ('Wq', 'bq', 'Wk', 'bk', 'Wv', 'bv', 'Wo', 'bo')}
    del _L0_xattn_all

    def _L0_ffn_setup():
        import jax, jax.numpy as jnp
        import numpy as np
        TOP_K = 2
        key = jax.random.key(seed)
        ks = jax.random.split(key, 6)
        B, S, H, F, E = (4, 256, 128, 512, 8)
        x = jax.random.normal(ks[0], (B, S, H), dtype=jnp.float32)
        Wg = jax.random.normal(ks[1], (H, E), dtype=jnp.float32) * (1.0 / np.sqrt(H))
        W1 = jax.random.normal(ks[2], (E, H, F), dtype=jnp.float32) * (1.0 / np.sqrt(H))
        b1 = jnp.zeros((E, F), dtype=jnp.float32)
        W2 = jax.random.normal(ks[3], (E, F, H), dtype=jnp.float32) * (1.0 / np.sqrt(F))
        b2 = jnp.zeros((E, H), dtype=jnp.float32)
        return {'x': x, 'Wg': Wg, 'W1': W1, 'b1': b1, 'W2': W2, 'b2': b2}
    _L0_ffn_all = _L0_ffn_setup()
    _L0_ffn_in = {k: v for k, v in _L0_ffn_all.items() if k in ('Wg', 'W1', 'b1', 'W2', 'b2')}
    del _L0_ffn_all

    def _L1_attn_setup():
        import jax, jax.numpy as jnp
        import numpy as np
        NUM_HEADS = 16
        key = jax.random.key(seed)
        k1, k2, k3 = jax.random.split(key, 3)
        S, B, E = (256, 4, 128)
        std = float(np.sqrt(2.0 / (E + E)))
        query = jax.random.normal(k1, (S, B, E), dtype=jnp.float32)
        in_proj_weight = jax.random.normal(k2, (3 * E, E), dtype=jnp.float32) * std
        in_proj_bias = jnp.zeros((3 * E,), dtype=jnp.float32)
        out_proj_weight = jax.random.normal(k3, (E, E), dtype=jnp.float32) * std
        out_proj_bias = jnp.zeros((E,), dtype=jnp.float32)
        return {'query': query, 'in_proj_weight': in_proj_weight, 'in_proj_bias': in_proj_bias, 'out_proj_weight': out_proj_weight, 'out_proj_bias': out_proj_bias}
    _L1_attn_all = _L1_attn_setup()
    _L1_attn_in = {k: v for k, v in _L1_attn_all.items() if k in ('in_proj_weight', 'in_proj_bias', 'out_proj_weight', 'out_proj_bias')}
    del _L1_attn_all

    def _L1_xattn_setup():
        import jax, jax.numpy as jnp
        import numpy as np
        QUERY_DIM = 128
        KEY_DIM = 96
        NUM_HEADS = 16
        HEAD_DIM = QUERY_DIM // NUM_HEADS
        SCALE = HEAD_DIM ** (-0.5)
        key = jax.random.key(seed)
        ks = jax.random.split(key, 11)
        B, Nq, Nk = (4, 512, 128)
        s_q = QUERY_DIM ** (-0.5)
        s_k = KEY_DIM ** (-0.5)
        return {'query': jax.random.normal(ks[0], (B, Nq, QUERY_DIM), jnp.float32), 'key': jax.random.normal(ks[1], (B, Nk, KEY_DIM), jnp.float32), 'value': jax.random.normal(ks[2], (B, Nk, KEY_DIM), jnp.float32), 'Wq': jax.random.normal(ks[3], (QUERY_DIM, QUERY_DIM), jnp.float32) * s_q, 'bq': jnp.zeros((QUERY_DIM,), jnp.float32), 'Wk': jax.random.normal(ks[4], (KEY_DIM, QUERY_DIM), jnp.float32) * s_k, 'bk': jnp.zeros((QUERY_DIM,), jnp.float32), 'Wv': jax.random.normal(ks[5], (KEY_DIM, QUERY_DIM), jnp.float32) * s_k, 'bv': jnp.zeros((QUERY_DIM,), jnp.float32), 'Wo': jax.random.normal(ks[6], (QUERY_DIM, QUERY_DIM), jnp.float32) * s_q, 'bo': jnp.zeros((QUERY_DIM,), jnp.float32)}
    _L1_xattn_all = _L1_xattn_setup()
    _L1_xattn_in = {k: v for k, v in _L1_xattn_all.items() if k in ('Wq', 'bq', 'Wk', 'bk', 'Wv', 'bv', 'Wo', 'bo')}
    del _L1_xattn_all

    def _L1_ffn_setup():
        import jax, jax.numpy as jnp
        import numpy as np
        D_MODEL, D_FF, N_EXPERTS, TOP_K = (128, 256, 8, 2)
        B, S = (2, 256)
        key = jax.random.key(seed)
        ks = jax.random.split(key, 6)
        sd = 1.0 / np.sqrt(D_MODEL)
        sf = 1.0 / np.sqrt(D_FF)
        return {'x': jax.random.normal(ks[0], (B, S, D_MODEL), jnp.float32), 'router_w': jax.random.normal(ks[1], (N_EXPERTS, D_MODEL), jnp.float32) * sd, 'gate_w': jax.random.normal(ks[2], (N_EXPERTS, D_MODEL, D_FF), jnp.float32) * sd, 'gate_b': jnp.zeros((N_EXPERTS, D_FF), jnp.float32), 'up_w': jax.random.normal(ks[3], (N_EXPERTS, D_MODEL, D_FF), jnp.float32) * sd, 'up_b': jnp.zeros((N_EXPERTS, D_FF), jnp.float32), 'down_w': jax.random.normal(ks[4], (N_EXPERTS, D_FF, D_MODEL), jnp.float32) * sf, 'down_b': jnp.zeros((N_EXPERTS, D_MODEL), jnp.float32)}
    _L1_ffn_all = _L1_ffn_setup()
    _L1_ffn_in = {k: v for k, v in _L1_ffn_all.items() if k in ('router_w', 'gate_w', 'gate_b', 'up_w', 'up_b', 'down_w', 'down_b')}
    del _L1_ffn_all
    return {'x': x, 'ctx_768': ctx_768, 'L0_attn_W_in': _L0_attn_in['W_in'], 'L0_attn_conv_w': _L0_attn_in['conv_w'], 'L0_attn_conv_b': _L0_attn_in['conv_b'], 'L0_attn_W_x': _L0_attn_in['W_x'], 'L0_attn_W_dt': _L0_attn_in['W_dt'], 'L0_attn_b_dt': _L0_attn_in['b_dt'], 'L0_attn_A_log': _L0_attn_in['A_log'], 'L0_attn_D': _L0_attn_in['D'], 'L0_attn_W_out': _L0_attn_in['W_out'], 'L0_xattn_Wq': _L0_xattn_in['Wq'], 'L0_xattn_bq': _L0_xattn_in['bq'], 'L0_xattn_Wk': _L0_xattn_in['Wk'], 'L0_xattn_bk': _L0_xattn_in['bk'], 'L0_xattn_Wv': _L0_xattn_in['Wv'], 'L0_xattn_bv': _L0_xattn_in['bv'], 'L0_xattn_Wo': _L0_xattn_in['Wo'], 'L0_xattn_bo': _L0_xattn_in['bo'], 'L0_ffn_Wg': _L0_ffn_in['Wg'], 'L0_ffn_W1': _L0_ffn_in['W1'], 'L0_ffn_b1': _L0_ffn_in['b1'], 'L0_ffn_W2': _L0_ffn_in['W2'], 'L0_ffn_b2': _L0_ffn_in['b2'], 'L1_attn_in_proj_weight': _L1_attn_in['in_proj_weight'], 'L1_attn_in_proj_bias': _L1_attn_in['in_proj_bias'], 'L1_attn_out_proj_weight': _L1_attn_in['out_proj_weight'], 'L1_attn_out_proj_bias': _L1_attn_in['out_proj_bias'], 'L1_xattn_Wq': _L1_xattn_in['Wq'], 'L1_xattn_bq': _L1_xattn_in['bq'], 'L1_xattn_Wk': _L1_xattn_in['Wk'], 'L1_xattn_bk': _L1_xattn_in['bk'], 'L1_xattn_Wv': _L1_xattn_in['Wv'], 'L1_xattn_bv': _L1_xattn_in['bv'], 'L1_xattn_Wo': _L1_xattn_in['Wo'], 'L1_xattn_bo': _L1_xattn_in['bo'], 'L1_ffn_router_w': _L1_ffn_in['router_w'], 'L1_ffn_gate_w': _L1_ffn_in['gate_w'], 'L1_ffn_gate_b': _L1_ffn_in['gate_b'], 'L1_ffn_up_w': _L1_ffn_in['up_w'], 'L1_ffn_up_b': _L1_ffn_in['up_b'], 'L1_ffn_down_w': _L1_ffn_in['down_w'], 'L1_ffn_down_b': _L1_ffn_in['down_b']}

def reference(x, ctx_768, L0_attn_W_in, L0_attn_conv_w, L0_attn_conv_b, L0_attn_W_x, L0_attn_W_dt, L0_attn_b_dt, L0_attn_A_log, L0_attn_D, L0_attn_W_out, L0_xattn_Wq, L0_xattn_bq, L0_xattn_Wk, L0_xattn_bk, L0_xattn_Wv, L0_xattn_bv, L0_xattn_Wo, L0_xattn_bo, L0_ffn_Wg, L0_ffn_W1, L0_ffn_b1, L0_ffn_W2, L0_ffn_b2, L1_attn_in_proj_weight, L1_attn_in_proj_bias, L1_attn_out_proj_weight, L1_attn_out_proj_bias, L1_xattn_Wq, L1_xattn_bq, L1_xattn_Wk, L1_xattn_bk, L1_xattn_Wv, L1_xattn_bv, L1_xattn_Wo, L1_xattn_bo, L1_ffn_router_w, L1_ffn_gate_w, L1_ffn_gate_b, L1_ffn_up_w, L1_ffn_up_b, L1_ffn_down_w, L1_ffn_down_b):
    import jax
    import jax.numpy as jnp

    def _L0_attn_ref(x, W_in, conv_w, conv_b, W_x, W_dt, b_dt, A_log, D, W_out):
        import math
        import jax, jax.numpy as jnp
        import numpy as np
        D_MODEL = 128
        D_STATE = 16
        D_CONV = 4
        EXPAND = 2
        D_INNER = EXPAND * D_MODEL
        DT_RANK = math.ceil(D_MODEL / 16)
        BATCH, SEQ = (1, 256)
        DT_MIN, DT_MAX, DT_FLOOR = (0.001, 0.1, 0.0001)

        def _mamba(x, W_in, conv_w, conv_b, W_x, W_dt, b_dt, A_log, D, W_out):
            B, L, _ = x.shape
            xz = x @ W_in.T
            xs, z = jnp.split(xz, 2, axis=-1)
            xc = jnp.pad(xs.transpose(0, 2, 1), ((0, 0), (0, 0), (D_CONV - 1, 0)))
            xc = jax.lax.conv_general_dilated(xc, conv_w, (1,), 'VALID', dimension_numbers=('NCH', 'OIH', 'NCH'), feature_group_count=D_INNER)
            xs = jax.nn.silu(xc.transpose(0, 2, 1) + conv_b[None, None, :])
            A = -jnp.exp(A_log)
            x_dbl = xs @ W_x.T
            dt, Bm, Cm = jnp.split(x_dbl, [DT_RANK, DT_RANK + D_STATE], axis=-1)
            dt = jax.nn.softplus(dt @ W_dt.T + b_dt)
            dA = jnp.exp(dt[..., None] * A)
            dBx = dt[..., None] * Bm[:, :, None, :] * xs[..., None]

            def step(h, inputs):
                dA_t, dBx_t, C_t = inputs
                h = dA_t * h + dBx_t
                y = jnp.einsum('bdn,bn->bd', h, C_t)
                return (h, y)
            h0 = jnp.zeros((B, D_INNER, D_STATE), xs.dtype)
            _, ys = jax.lax.scan(step, h0, (dA.transpose(1, 0, 2, 3), dBx.transpose(1, 0, 2, 3), Cm.transpose(1, 0, 2)))
            y = ys.transpose(1, 0, 2) + xs * D
            return y * jax.nn.silu(z) @ W_out.T
        return _mamba(x, W_in, conv_w, conv_b, W_x, W_dt, b_dt, A_log, D, W_out)

    def _L0_xattn_ref(query, key_value, Wq, bq, Wk, bk, Wv, bv, Wo, bo):
        import jax, jax.numpy as jnp
        import numpy as np
        NUM_HEADS = 16
        CLAMP = 10000.0
        B, Nq, Cq = query.shape
        Nkv = key_value.shape[1]
        H = NUM_HEADS
        D = Cq // H
        scale = D ** (-0.5)
        q = (query @ Wq + bq).reshape(B, Nq, H, D).transpose(0, 2, 1, 3)
        k = (key_value @ Wk + bk).reshape(B, Nkv, H, D).transpose(0, 2, 1, 3)
        v = (key_value @ Wv + bv).reshape(B, Nkv, H, D).transpose(0, 2, 1, 3)
        attn = jnp.einsum('bhqd,bhkd->bhqk', q, k) * scale
        attn = jnp.clip(attn, -CLAMP, CLAMP)
        attn = jax.nn.softmax(attn, axis=-1)
        attn = jnp.where(jnp.any(jnp.isnan(attn)), jnp.asarray(1.0 / Nkv, attn.dtype), attn)
        x = jnp.einsum('bhqk,bhkd->bqhd', attn, v).reshape(B, Nq, Cq)
        return x @ Wo + bo

    def _L0_ffn_ref(x, Wg, W1, b1, W2, b2):
        import jax, jax.numpy as jnp
        import numpy as np
        TOP_K = 2
        B, S, H = x.shape
        xt = x.reshape(-1, H)
        T = xt.shape[0]
        logits = xt @ Wg
        probs = jax.nn.softmax(logits, axis=-1)
        topk_p, topk_i = jax.lax.top_k(probs, TOP_K)
        topk_p = topk_p / jnp.sum(topk_p, axis=-1, keepdims=True)
        combine = jnp.zeros_like(probs).at[jnp.arange(T)[:, None], topk_i].set(topk_p)
        h = jax.nn.gelu(jnp.einsum('th,ehf->tef', xt, W1) + b1)
        eo = jnp.einsum('tef,efh->teh', h, W2) + b2
        out = jnp.einsum('te,teh->th', combine, eo)
        return out.reshape(B, S, H)

    def _L1_attn_ref(query, in_proj_weight, in_proj_bias, out_proj_weight, out_proj_bias):
        import jax, jax.numpy as jnp
        import numpy as np
        NUM_HEADS = 16
        S, B, E = query.shape
        H = NUM_HEADS
        hd = E // H
        scale = hd ** (-0.5)
        lin = jnp.einsum('sbe,fe->sbf', query, in_proj_weight) + in_proj_bias
        lin = lin.reshape(S, B * H, 3, hd)
        q = lin[:, :, 0, :]
        k = lin[:, :, 1, :]
        v = lin[:, :, 2, :]
        scores = jnp.einsum('sbd,tbd->bst', q, k) * scale
        attn = jax.nn.softmax(scores.astype(jnp.float32), axis=-1).astype(scores.dtype)
        ctx = jnp.einsum('bst,tbd->sbd', attn, v).reshape(S, B, E)
        out = jnp.einsum('sbe,fe->sbf', ctx, out_proj_weight) + out_proj_bias
        return out

    def _L1_xattn_ref(query, key, value, Wq, bq, Wk, bk, Wv, bv, Wo, bo):
        import jax, jax.numpy as jnp
        import numpy as np
        QUERY_DIM = 128
        KEY_DIM = 96
        NUM_HEADS = 16
        HEAD_DIM = QUERY_DIM // NUM_HEADS
        SCALE = HEAD_DIM ** (-0.5)
        B, Nq, _ = query.shape
        Nk = key.shape[1]
        q = (query @ Wq + bq).reshape(B, Nq, NUM_HEADS, HEAD_DIM).transpose(0, 2, 1, 3)
        k = (key @ Wk + bk).reshape(B, Nk, NUM_HEADS, HEAD_DIM).transpose(0, 2, 1, 3)
        v = (value @ Wv + bv).reshape(B, Nk, NUM_HEADS, HEAD_DIM).transpose(0, 2, 1, 3)
        attn = jnp.einsum('bhqd,bhkd->bhqk', q, k) * SCALE
        attn = jax.nn.softmax(attn, axis=-1)
        out = jnp.einsum('bhqk,bhkd->bhqd', attn, v)
        out = out.transpose(0, 2, 1, 3).reshape(B, Nq, QUERY_DIM)
        return out @ Wo + bo

    def _L1_ffn_ref(x, router_w, gate_w, gate_b, up_w, up_b, down_w, down_b):
        import jax, jax.numpy as jnp
        import numpy as np
        D_MODEL, D_FF, N_EXPERTS, TOP_K = (128, 256, 8, 2)
        B, S = (2, 256)
        b, s, d = x.shape
        xf = x.reshape(b * s, d)
        n = xf.shape[0]
        router_logits = xf @ router_w.T
        probs = jax.nn.softmax(router_logits, axis=-1)
        topv, topi = jax.lax.top_k(probs, TOP_K)
        mask = jnp.zeros_like(probs).at[jnp.arange(n)[:, None], topi].set(1.0)
        probs = probs * mask
        probs = probs / (probs.sum(axis=-1, keepdims=True) + 1e-09)
        g = jnp.einsum('nd,edf->nef', xf, gate_w) + gate_b
        u = jnp.einsum('nd,edf->nef', xf, up_w) + up_b
        h = jax.nn.silu(g) * u
        expert_out = jnp.einsum('nef,efd->ned', h, down_w) + down_b
        y = jnp.einsum('ne,ned->nd', probs, expert_out)
        return y.reshape(b, s, d)
    x = x + _L0_attn_ref(_layernorm(x, axis=-1), L0_attn_W_in, L0_attn_conv_w, L0_attn_conv_b, L0_attn_W_x, L0_attn_W_dt, L0_attn_b_dt, L0_attn_A_log, L0_attn_D, L0_attn_W_out)
    x = x + _L0_xattn_ref(_layernorm(x, axis=-1), ctx_768, L0_xattn_Wq, L0_xattn_bq, L0_xattn_Wk, L0_xattn_bk, L0_xattn_Wv, L0_xattn_bv, L0_xattn_Wo, L0_xattn_bo)
    x = x + _L0_ffn_ref(_layernorm(x, axis=-1), L0_ffn_Wg, L0_ffn_W1, L0_ffn_b1, L0_ffn_W2, L0_ffn_b2)
    x = x + _L1_attn_ref(_layernorm(x, axis=-1), L1_attn_in_proj_weight, L1_attn_in_proj_bias, L1_attn_out_proj_weight, L1_attn_out_proj_bias)
    x = x + _L1_xattn_ref(_layernorm(x, axis=-1), ctx_768, ctx_768, L1_xattn_Wq, L1_xattn_bq, L1_xattn_Wk, L1_xattn_bk, L1_xattn_Wv, L1_xattn_bv, L1_xattn_Wo, L1_xattn_bo)
    x = x + _L1_ffn_ref(_layernorm(x, axis=-1), L1_ffn_router_w, L1_ffn_gate_w, L1_ffn_gate_b, L1_ffn_up_w, L1_ffn_up_b, L1_ffn_down_w, L1_ffn_down_b)
    return x

_drawn_inputs = setup_inputs


def setup_inputs(seed=0):
    import zlib

    import numpy as np

    out = dict(_drawn_inputs(seed))
    spreads = {'L0_attn_conv_b': (0.0, 0.1),
     'L0_attn_D': (1.0, 0.2),
     'L0_xattn_bq': (0.0, 0.1),
     'L0_xattn_bk': (0.0, 0.8),
     'L0_xattn_bv': (0.0, 0.1),
     'L0_xattn_bo': (0.0, 0.1),
     'L0_ffn_b1': (0.0, 0.1),
     'L0_ffn_b2': (0.0, 0.1),
     'L1_attn_in_proj_bias': (0.0, 0.1),
     'L1_attn_out_proj_bias': (0.0, 0.1),
     'L1_xattn_bq': (0.0, 0.1),
     'L1_xattn_bk': (0.0, 0.8),
     'L1_xattn_bv': (0.0, 0.1),
     'L1_xattn_bo': (0.0, 0.1),
     'L1_ffn_gate_b': (0.0, 0.268),
     'L1_ffn_up_b': (0.0, 0.268),
     'L1_ffn_down_b': (0.0, 0.1)}
    factors = {}
    for name, (base, spread) in spreads.items():
        noise = np.random.default_rng([zlib.crc32(name.encode()), seed]).standard_normal(out[name].shape)
        drawn = base * np.exp(spread * noise) if base else spread * noise
        out[name] = jnp.asarray(drawn.astype(out[name].dtype))
    for name, factor in factors.items():
        out[name] = (out[name] * factor).astype(out[name].dtype)
    return out
```

```python
import numpy as np
from contextlib import ExitStack

import concourse.bass as bass
from concourse import mybir

BATCH, SEQ, D, DC = 64, 64, 128, 96
TOKENS = BATCH * SEQ
P = 128
GROUP = 512
TILES = GROUP // P
GROUPS = TOKENS // GROUP
EXPERTS = 8
HEADS, HD = 16, 8
LN_EPS = 1e-5

F32 = mybir.dt.float32
BF16 = mybir.dt.bfloat16
I32 = mybir.dt.int32
ALU = mybir.AluOpType
ACT = mybir.ActivationFunctionType
AX = mybir.AxisListType


class Count:

    def __init__(self, sem, base=0):
        self.sem, self.base, self.n = sem, base, 0

    def at(self, n):
        return self.base + n

    def __call__(self, ins):
        ins.then_inc(self.sem, 1)
        self.n += 1
        return ins


def linker(eng, count):
    def link(ins):
        count(ins)
        eng.wait_ge(count.sem, count.at(count.n))
        return ins
    return link


def bc(ap, axis, n):
    ap = ap.unsqueeze(axis)
    shape = list(ap.shape)
    shape[axis] = n
    return ap.broadcast_to(shape)


def rows(dram, g):
    return dram.rearrange("(n p) d -> p n d", p=P)[:, bass.ds(g * TILES, TILES), :]


class Memory:

    def __init__(self, nc, ctx, prefix):
        self.nc, self.ctx, self.prefix = nc, ctx, prefix
        self.sems = []

    def sb(self, name, shape, dt=F32):
        return self.ctx.enter_context(self.nc.sbuf_tensor(f"{self.prefix}_{name}", shape, dt))

    def ps(self, name, shape):
        return self.ctx.enter_context(self.nc.psum_tensor(f"{self.prefix}_{name}", shape, F32))

    def sem(self, name):
        self.sems.append(self.nc.alloc_semaphore(name=f"{self.prefix}_{name}"))
        return self.sems[-1]

    def clear(self):
        self.nc.clear_and_free_semaphores(self.sems)
        self.nc.all_engine_barrier()


class LayerNorm:

    LINKS = 3

    def __init__(self, m):
        self.stats = m.sb("stats", [P, TILES, 6])
        self.sum = m.sb("ln_sum", [P, TILES])
        self.mean = m.sb("ln_mean", [P, TILES])
        self.diff = m.sb("ln_diff", [P, TILES])
        self.m2 = m.sb("ln_m2", [P, TILES])
        self.dm2 = m.sb("ln_dm2", [P, TILES])
        self.var_eps = m.sb("ln_var_eps", [P, TILES])
        self.rstd = m.sb("ln_rstd", [P, TILES])
        self.minus_half = m.sb("ln_minus_half", [P, TILES])


def layer_norm_stats(v, link, x, ln):
    for t in range(TILES):
        ins = v.bn_stats(ln.stats[:, t, :], x[:, t, :])
    link(ins)
    v.tensor_tensor(ln.sum[:, :], ln.stats[:, :, 1], ln.stats[:, :, 4], ALU.add)
    v.tensor_tensor(ln.diff[:, :], ln.stats[:, :, 1], ln.stats[:, :, 4], ALU.subtract)
    link(v.tensor_tensor(ln.m2[:, :], ln.stats[:, :, 2], ln.stats[:, :, 5], ALU.add))
    v.tensor_scalar(ln.mean[:, :], ln.sum[:, :], 0.5, None, ALU.mult)
    v.tensor_scalar(ln.m2[:, :], ln.m2[:, :], 1.0 / D, LN_EPS, ALU.mult, ALU.add)
    link(v.scalar_tensor_tensor(ln.dm2[:, :], ln.diff[:, :], 0.25, ln.diff[:, :], ALU.mult, ALU.mult))


def layer_norm_apply(v, x, ln, xn):
    for t in range(TILES):
        ins = v.tensor_scalar(xn[:, t, :], x[:, t, :], ln.mean[:, t:t + 1], ln.rstd[:, t:t + 1],
                              ALU.subtract, ALU.mult)
    return ins


def reach(eng, sem, value):
    if not (isinstance(value, int) and value <= 0):
        eng.wait_ge(sem, value)


def everything(t):
    return t[tuple(slice(None) for _ in t.shape)]


def sequence_rows(dram, half, g, n):
    return dram.rearrange("(s t u) d -> u s t d", u=2, t=BATCH // 2)[half, :, bass.ds(g * TILES, n * TILES), :]


def attention_phase(nc, pre, w, src, dst, ctxT, self_attn=False, guarded=False):
    CLAMP = 10000.0
    C = D if self_attn else DC
    UNITS = 8
    SLOTS = 2 * UNITS
    STEPS = GROUPS // 2
    KEYS = SEQ
    SCALE = float(HD) ** -0.5
    HALF = P // 2
    with ExitStack() as ctx:
        m = Memory(nc, ctx, pre)
        ctx.callback(m.clear)
        wq = m.sb("wq", [D, P])
        wk = m.sb("wk", [C, P])
        wv = m.sb("wv", [C, 2, HALF])
        wo = m.sb("wo", [P, D])
        bq = m.sb("bq", [P, 1])
        bk = m.sb("bk", [P, 1])
        bv = m.sb("bv", [P, HALF])
        bo = m.sb("bo", [P, D])
        bq_scaled = m.sb("bq_scaled", [P, 1])
        bk_masked = m.sb("bk_masked", [P, 4])
        mask = m.sb("mask", [P, 4])
        ident = m.sb("ident", [P, P])
        x = m.sb("x", [P, GROUPS * TILES, D])
        kv = None if self_attn else m.sb("kv", [C, TOKENS])
        kvg = None if self_attn else m.sb("kvg", [C, GROUP])
        ln = LayerNorm(m)
        xn = m.sb("xn", [P, TILES, D])
        xnT = m.sb("xnT", [D, GROUP])
        qT = m.sb("qT", [P, 2, GROUP])
        kT = m.sb("kT", [P, 2, 4, GROUP])
        v1 = m.sb("v1", [P, 2, TILES, HEADS // 2, 2, 2 * HD])
        ot_sb = m.sb("ot_sb", [P, 2, GROUP // 2])
        smax = m.sb("smax", [P, 4, 8])
        s_clip = m.sb("s_clip", [P, 4, GROUP]) if guarded else None
        s_sb = m.sb("s_sb", [P, 4, GROUP])
        pt_sb = m.sb("pt_sb", [P, 2, GROUP])
        rden = m.sb("rden", [P, 2, HEADS])
        on = m.sb("on", [P, 2, TILES, D])
        oT = m.sb("oT", [P, TOKENS if guarded else GROUP])

        pS = m.ps("pS", [P, 2, GROUP])
        pPT = m.ps("pPT", [P, GROUP])
        pOT = m.ps("pOT", [P, GROUP // 2])
        pO = m.ps("pO", [P, 2, GROUP])
        pM = m.ps("pM", [P, 2, GROUP])

        w_in, x_first, x_rest, kv_in = m.sem("w_in"), m.sem("x_first"), m.sem("x_rest"), m.sem("kv_in")
        consts, setup = m.sem("consts"), m.sem("setup")
        var_ready, rstd_ready, xn_ready = m.sem("var_ready"), m.sem("rstd_ready"), m.sem("xn_ready")
        xT_psum, xnT_ready, kvg_ready = m.sem("xT_psum"), m.sem("xnT_ready"), m.sem("kvg_ready")
        k_psum, k_ready, q_psum, q_ready = m.sem("k_psum"), m.sem("k_ready"), m.sem("q_psum"), m.sem("q_ready")
        v_psum, v_ready, xb_ready = m.sem("v_psum"), m.sem("v_ready"), m.sem("xb_ready")
        s_psum, clip_done, max_done, s_used = m.sem("s_psum"), m.sem("clip_done"), m.sem("max_done"), m.sem("s_used")
        exp_done, pt_psum, pt_ready = m.sem("exp_done"), m.sem("pt_psum"), m.sem("pt_ready")
        pv_psum, po_ready, o_psum = m.sem("pv_psum"), m.sem("po_ready"), m.sem("o_psum")
        o_used, rden_done = m.sem("o_used"), m.sem("rden_done")
        ot_psum, ot_ready, y_psum, y_done = m.sem("ot_psum"), m.sem("ot_ready"), m.sem("y_psum"), m.sem("y_done")
        x_out, chain, guard = m.sem("x_out"), m.sem("chain"), m.sem("guard")
        flag_psum = m.sem("flag_psum")

        block = ctx.enter_context(nc.Block())
        NW = 11

        if guarded:
            nan_sum = m.sb("nan_sum", [P, 2 * GROUPS])
            nan_col = m.sb("nan_col", [P, 4])
            nan_mask = m.sb("nan_mask", [P, 1])
            ones = m.sb("ones", [P, P])
            kv_mean = m.sb("kv_mean", [C, BATCH])
            wv_all = m.sb("wv_all", [C, P])
            bv_col = m.sb("bv_col", [P, 1])
            v_mean = m.sb("v_mean", [P, BATCH])
            NW += 2

        def two_groups(eng, step):
            step(0, True, False)
            with eng.Fori(1, STEPS - 1) as i:
                step(i, False, False)
            step(STEPS - 1, False, True)

        def at_most(count):
            return min(count, GROUPS) if isinstance(count, int) else count

        def xg(g):
            return x[:, bass.ds(g * TILES, TILES), :]

        @block.sync
        def _(sp):
            def load(g, n, sem):
                if self_attn:
                    for half in range(2):
                        sp.dma_start(x[half * HALF:(half + 1) * HALF, g * TILES:(g + n) * TILES, :],
                                     sequence_rows(src, half, g, n)).then_inc(sem, 16)
                else:
                    sp.dma_start(x[:, g * TILES:(g + n) * TILES, :],
                                 src.rearrange("(n p) d -> p n d", p=P)[:, g * TILES:(g + n) * TILES, :]
                                 ).then_inc(sem, 16)

            load(0, 1, x_first)
            if not self_attn:
                sp.dma_start(kv[:, :], ctxT).then_inc(kv_in, 16)
            loads = [(ident, "ident"), (wq, pre + "_wq"), (wk, pre + "_wk"), (wv, pre + "_wv"), (wo, pre + "_wo"),
                     (bq, pre + "_bq"), (bk, pre + "_bk"), (mask, "mask")]
            if guarded:
                loads += [(wv_all, pre + "_wv_all"), (bv_col, pre + "_bv_col")]
            for buf, name in loads:
                sp.dma_start(everything(buf), w[name]).then_inc(w_in, 16)
            for half in range(2):
                sp.dma_start(bv[half * HALF:(half + 1) * HALF, :],
                             w[pre + "_bv"][half].partition_broadcast(HALF)).then_inc(w_in, 16)
            sp.dma_start(bo[:, :], w[pre + "_bo"].partition_broadcast(P)).then_inc(w_in, 16)
            load(1, GROUPS - 1, x_rest)

            def store(g):
                sp.wait_ge(y_done, g + 1)
                if self_attn:
                    for half in range(2):
                        sp.dma_start(sequence_rows(dst, half, g, 1),
                                     x[half * HALF:(half + 1) * HALF, bass.ds(g * TILES, TILES), :]
                                     ).then_inc(x_out, 16)
                else:
                    sp.dma_start(rows(dst, g), xg(g)).then_inc(x_out, 16)

            sp.wait_ge(x_first, 16 * (2 if self_attn else 1))
            sp.wait_ge(x_rest, 16 * (2 if self_attn else 1))
            with sp.Fori(0, GROUPS) as g:
                store(g)
            sp.wait_ge(x_out, 16 * GROUPS * (2 if self_attn else 1))

        @block.gpsimd
        def _(pool):
            pool.memset(ln.minus_half[:, :], -0.5).then_inc(consts, 1)
            pool.memset(everything(v1), 1.0).then_inc(consts, 1)
            if guarded:
                pool.memset(ones[:, :], 1.0).then_inc(consts, 1)
            pool.wait_ge(consts, 3 if guarded else 2)
            pool.wait_ge(w_in, 16 * NW)

            def rstd(g):
                pool.wait_ge(var_ready, g + 1)
                pool.tensor_tensor(ln.rstd[:, :], ln.var_eps[:, :], ln.minus_half[:, :],
                                   ALU.pow).then_inc(rstd_ready, 1)

            def add_bias(g):
                pool.wait_ge(xn_ready, g + 1)
                pool.tensor_tensor(xg(g), xg(g), bc(bo[:, :], 1, TILES), ALU.add).then_inc(xb_ready, 1)

            def subtract_max(n, s):
                pool.wait_ge(max_done, n + 1)
                reach(pool, pt_psum, n - 3)
                pool.tensor_tensor(s_sb[:, s % 4, :].rearrange("p (h k) -> p h k", k=KEYS),
                                   s_clip[:, s % 4, :].rearrange("p (h k) -> p h k", k=KEYS),
                                   bc(smax[:, s % 4, :], 2, KEYS), ALU.subtract).then_inc(s_used, 1)

            rstd(0)
            rstd(1)
            add_bias(0)

            def step(i, first, last):
                for s in range(SLOTS):
                    c, u = 2 * i + s // UNITS, s % UNITS
                    if guarded:
                        subtract_max(i * SLOTS + s, s)
                    if u == 5 and not last:
                        rstd(c + 2)
                    if u == 6 and not (last and s >= UNITS):
                        add_bias(c + 1)
            two_groups(pool, step)

        @block.vector
        def _(v):
            v.wait_ge(w_in, 16 * NW)
            v.wait_ge(consts, 3 if guarded else 2)
            link = linker(v, Count(chain, 0))
            v.tensor_scalar(bq_scaled[:, :], bq[:, :], SCALE, None, ALU.mult)
            v.tensor_scalar(bk_masked[:, :], mask[:, :], bk[:, 0:1], None, ALU.mult).then_inc(setup, 1)
            if guarded:
                v.wait_ge(kv_in, 16)
                kv_sum = v.tensor_reduce(kv_mean[:, :], kv[:, :].rearrange("c (b k) -> c b k", k=KEYS), AX.X, ALU.add)
                link(kv_sum)
                v.tensor_scalar(kv_mean[:, :], kv_mean[:, :], 1.0 / KEYS, None, ALU.mult).then_inc(guard, 1)

            def layer_norm(g, link):
                if isinstance(g, int) and g == 0:
                    v.wait_ge(x_first, 16 * (2 if self_attn else 1))
                elif isinstance(g, int) and g == 1:
                    v.wait_ge(x_rest, 16 * (2 if self_attn else 1))
                layer_norm_stats(v, link, xg(g), ln)
                v.tensor_tensor(ln.var_eps[:, :], ln.m2[:, :], ln.dm2[:, :], ALU.add).then_inc(var_ready, 1)
                reach(v, xT_psum, g)
                v.wait_ge(rstd_ready, g + 1)
                layer_norm_apply(v, xg(g), ln, xn).then_inc(xn_ready, 1)
                v.wait_ge(xn_ready, g + 1)

            def value_bias(g, par):
                v.wait_ge(v_psum, g + 1)
                reach(v, pv_psum, (g - 1) * UNITS)
                for b in range(2):
                    ins = v.tensor_tensor(v1[:, par, :, :, b, 0:HD],
                                          pM[:, 1, :].rearrange("p (t b i d) -> p t b i d", b=2, i=HEADS // 2,
                                                                d=HD)[:, :, b],
                                          bc(bv[:, :], 1, TILES).rearrange("p t (i d) -> p t i d", d=HD), ALU.add)
                ins.then_inc(v_ready, 1)

            def scores(n, s):
                v.wait_ge(s_psum, n + 1)
                sc = pS[:, s % 2, :]
                if guarded:
                    reach(v, s_used, n - 3)
                    v.tensor_scalar(s_clip[:, s % 4, :], sc, -CLAMP, CLAMP, ALU.max, ALU.min).then_inc(clip_done, 1)
                    v.wait_ge(clip_done, n + 1)
                    v.tensor_reduce(smax[:, s % 4, :], s_clip[:, s % 4, :].rearrange("p (h k) -> p h k", k=KEYS),
                                    AX.X, ALU.max).then_inc(max_done, 1)
                else:
                    v.tensor_reduce(smax[:, s % 4, :], sc.rearrange("p (h k) -> p h k", k=KEYS),
                                    AX.X, ALU.max).then_inc(max_done, 1)
                    v.wait_ge(max_done, n + 1)
                    reach(v, pt_psum, n - 3)
                    v.tensor_tensor(s_sb[:, s % 4, :].rearrange("p (h k) -> p h k", k=KEYS),
                                    sc.rearrange("p (h k) -> p h k", k=KEYS),
                                    bc(smax[:, s % 4, :], 2, KEYS), ALU.subtract).then_inc(s_used, 1)

            def normalise(pp, g, k, par):
                v.wait_ge(o_psum, (pp + 1) * 4)
                if k == 0:
                    reach(v, ot_psum, g - 1)
                for b in range(2):
                    lo, hi = b * HALF, (b + 1) * HALF
                    o = pO[lo:hi, :, :].rearrange("p t (h b d) -> p t h b d", h=HEADS, b=2)[:, :, :, b]
                    ins = v.reciprocal(rden[lo:hi, :, :], o[:, :, :, HD])
                ins.then_inc(rden_done, 1)
                v.wait_ge(rden_done, pp + 1)
                for b in range(2):
                    lo, hi = b * HALF, (b + 1) * HALF
                    o = pO[lo:hi, :, :].rearrange("p t (h b d) -> p t h b d", h=HEADS, b=2)[:, :, :, b]
                    ins = v.tensor_tensor(on[lo:hi, par, 2 * k:2 * k + 2, :].rearrange("p t (h d) -> p t h d", d=HD),
                                          o[:, :, :, 0:HD], bc(rden[lo:hi, :, :], 3, HD), ALU.mult)
                ins.then_inc(o_used, 1)

            def residual(g):
                v.wait_ge(xb_ready, g + 1)
                v.wait_ge(y_psum, g + 1)
                bank = 1
                v.tensor_tensor(xg(g), pM[:, bank, :].rearrange("p (t d) -> p t d", d=D), xg(g),
                                ALU.add).then_inc(y_done, 1)

            def nan_sums(g, par):
                v.wait_ge(q_ready, g + 1)
                v.tensor_reduce(nan_sum[:, bass.ds(2 * g, 1)], qT[:, par, :], AX.X, ALU.add)
                v.wait_ge(k_ready, g + 1)
                v.tensor_reduce(nan_sum[:, bass.ds(2 * g + 1, 1)], kT[:, par, 0, :], AX.X,
                                ALU.add).then_inc(guard, 1)

            base = 1 if guarded else 0
            count = Count(chain, base)
            link = linker(v, count)
            layer_norm(0, link)
            layer_norm(1, link)
            value_bias(0, 0)
            if guarded:
                nan_sums(0, 0)
            LINKS = ln.LINKS

            def step(i, first, last):
                for s in range(SLOTS):
                    half, u = s // UNITS, s % UNITS
                    c = 2 * i + half
                    n = i * SLOTS + s
                    scores(n, s)
                    if u in (3, 7) and not (first and s == 3):
                        if u == 7:
                            normalise(4 * i + s // 4 - 1, c, 0, half)
                        else:
                            normalise(4 * i + s // 4 - 1, c - 1, 1, 1 - half)
                    if u == 4 and not (last and half == 1):
                        value_bias(c + 1, 1 - half)
                        if guarded:
                            nan_sums(c + 1, 1 - half)
                    if u == 5 and not last:
                        link = linker(v, Count(chain, base + (c + 2) * LINKS))
                        layer_norm(c + 2, link)
                    if u == 7 and not (first and half == 0) and not guarded:
                        residual(c - 1)

            two_groups(v, step)
            normalise(2 * GROUPS - 1, GROUPS - 1, 1, 1)
            if not guarded:
                residual(GROUPS - 1)
            else:
                v.wait_ge(guard, 1 + GROUPS)
                v.tensor_scalar(nan_sum[:, :], nan_sum[:, :], 0.0, None, ALU.mult).then_inc(guard, 1)
                v.wait_ge(guard, 2 + GROUPS)
                v.tensor_reduce(nan_col[:, 0:1], nan_sum[:, :], AX.X, ALU.add).then_inc(guard, 1)
                v.wait_ge(flag_psum, 1)
                v.tensor_copy(nan_col[:, 1:2], pO[:, 0, 0:1]).then_inc(guard, 1)
                v.wait_ge(guard, 4 + GROUPS)
                v.tensor_tensor(nan_mask[:, :], nan_col[:, 1:2], nan_col[:, 1:2], ALU.not_equal)
                v.tensor_scalar(v_mean[:, :], pO[:, 1, 0:BATCH], bv_col[:, 0:1], None, ALU.add).then_inc(guard, 1)
                v.wait_ge(guard, 5 + GROUPS)
                v.wait_ge(ot_ready, GROUPS)
                v.copy_predicated(oT[:, :], bc(nan_mask[:, 0:1].bitcast(I32)[:, 0], 1, TOKENS),
                                  bc(v_mean[:, :], 2, KEYS)).then_inc(guard, 1)
                for g in range(GROUPS):
                    v.wait_ge(y_psum, g + 1)
                    v.wait_ge(xb_ready, g + 1)
                    v.tensor_tensor(xg(g), pM[:, g % 2, :].rearrange("p (t d) -> p t d", d=D), xg(g),
                                    ALU.add).then_inc(y_done, 1)

        @block.scalar
        def _(act):
            act.wait_ge(w_in, 16 * NW)
            act.wait_ge(setup, 1)

            def copy_xT(g):
                if self_attn:
                    reach(act, v_psum, g)
                reach(act, q_psum, g)
                act.wait_ge(xT_psum, g + 1)
                act.activation(xnT[:, :], pM[:, 0, :], ACT.Identity).then_inc(xnT_ready, 1)

            def copy_kv(g):
                if not self_attn:
                    act.wait_ge(kv_in, 16)
                    reach(act, v_psum, g)
                    act.activation(kvg[:, :], kv[:, bass.ds(g * GROUP, GROUP)], ACT.Identity).then_inc(kvg_ready, 1)

            def copy_k(g, par):
                act.wait_ge(k_psum, g + 1)
                reach(act, s_psum, (g - 1) * UNITS)
                if guarded:
                    reach(act, guard, g)
                for j in range(4):
                    ins = act.activation(kT[:, par, j, :], pM[:, 1, :], ACT.Identity, bias=bk_masked[:, j:j + 1],
                                         scale=mask[:, j:j + 1])
                ins.then_inc(k_ready, 1)

            def copy_q(g, par):
                act.wait_ge(q_psum, g + 1)
                reach(act, s_psum, (g - 1) * UNITS)
                if guarded:
                    reach(act, guard, g)
                act.activation(qT[:, par, :], pM[:, 0, :], ACT.Identity, bias=bq_scaled[:, 0:1],
                               scale=SCALE).then_inc(q_ready, 1)

            def exponent(n, s):
                act.wait_ge(s_used, n + 1)
                act.activation(s_sb[:, s % 4, :], s_sb[:, s % 4, :], ACT.Exp).then_inc(exp_done, 1)

            def copy_pt(n, s):
                act.wait_ge(pt_psum, n + 1)
                reach(act, pv_psum, n - 1)
                act.activation(pt_sb[:, s % 2, :], pPT[:, :], ACT.Identity).then_inc(pt_ready, 1)

            def copy_po(n, s):
                act.wait_ge(pv_psum, n + 1)
                reach(act, o_psum, n - 1)
                act.activation(ot_sb[:, s % 2, :], pOT[:, :], ACT.Identity).then_inc(po_ready, 1)

            def copy_oT(g):
                act.wait_ge(ot_psum, g + 1)
                if guarded:
                    out = oT[:, bass.ds(g * GROUP, GROUP)]
                else:
                    reach(act, y_psum, g)
                    out = oT[:, :]
                act.activation(out, pM[:, 0, :], ACT.Identity).then_inc(ot_ready, 1)

            copy_kv(0)
            copy_xT(0)
            copy_k(0, 0)
            copy_q(0, 0)
            if not self_attn:
                copy_kv(1)

            def step(i, first, last):
                for s in range(SLOTS):
                    half, u = s // UNITS, s % UNITS
                    c = 2 * i + half
                    n = i * SLOTS + s
                    if not (first and s < 1):
                        exponent(n - 1, s - 1)
                    if not (first and s < 2):
                        copy_pt(n - 2, s - 2)
                    if not (first and s < 3):
                        copy_po(n - 3, s - 3)
                    if not (last and half == 1):
                        if u == 0:
                            copy_xT(c + 1)
                        if u == 2:
                            copy_k(c + 1, 1 - half)
                        if u == 3:
                            copy_q(c + 1, 1 - half)
                        if u == 6 and not (last and half == 0) and not self_attn:
                            copy_kv(c + 2)
                    if u == 5 and not (first and half == 0):
                        copy_oT(c - 1)
            two_groups(act, step)
            N = GROUPS * UNITS
            exponent(N - 1, N - 1)
            copy_pt(N - 2, N - 2)
            copy_po(N - 3, N - 3)
            copy_pt(N - 1, N - 1)
            copy_po(N - 2, N - 2)
            copy_po(N - 1, N - 1)
            copy_oT(GROUPS - 1)

        @block.tensor
        def _(pe):
            pe.wait_ge(w_in, 16 * NW)
            pe.wait_ge(consts, 3 if guarded else 2)

            def turn_x(g):
                pe.wait_ge(xn_ready, g + 1)
                reach(pe, ot_ready, g - 2)
                for t in range(TILES):
                    ins = pe.transpose(pM[:, 0, t * P:(t + 1) * P], xn[:, t, :], ident[:, :])
                ins.then_inc(xT_psum, 1)

            def project_k(g):
                if self_attn:
                    pe.wait_ge(xnT_ready, g + 1)
                else:
                    pe.wait_ge(kvg_ready, g + 1)
                if guarded:
                    reach(pe, v_ready, g)
                else:
                    reach(pe, y_done, g - 2)
                    reach(pe, v_ready, g)
                pe.matmul(pM[:, 1, :], wk[:, :], (xnT if self_attn else kvg)[:, :],
                          start=True, stop=True).then_inc(k_psum, 1)

            def project_q(g):
                pe.wait_ge(xnT_ready, g + 1)
                pe.matmul(pM[:, 0, :], wq[:, :], xnT[:, :], start=True, stop=True).then_inc(q_psum, 1)

            def project_v(g):
                pe.wait_ge(k_ready, g + 1)
                kvT = xnT if self_attn else kvg
                for b in range(2 * TILES):
                    for hl in range(2):
                        ins = pe.matmul(pM[hl * HALF:(hl + 1) * HALF, 1, b * HALF:(b + 1) * HALF],
                                        kvT[:, b * SEQ:(b + 1) * SEQ], wv[:, hl, :], start=True, stop=True)
                ins.then_inc(v_psum, 1)

            def scores(n, s, par):
                pp, r = (s // 4) % 2, s % 4
                reach(pe, clip_done if guarded else s_used, n - 1)
                for pl in range(2):
                    for b in range(2):
                        t0 = (2 * pp + pl) * P + b * SEQ
                        ins = pe.matmul(pS[b * HALF:(b + 1) * HALF, s % 2, pl * 256:(pl + 1) * 256],
                                        qT[32 * r:32 * r + 32, par, t0:t0 + SEQ],
                                        kT[32 * r:32 * r + 32, par, :, t0:t0 + SEQ], start=True, stop=True)
                ins.then_inc(s_psum, 1)

            def turn_weights(n, s):
                pe.wait_ge(exp_done, n + 1)
                reach(pe, pt_ready, n)
                for k in range(4):
                    ins = pe.transpose(pPT[:, k * P:(k + 1) * P], s_sb[:, s % 4, k * P:(k + 1) * P],
                                       ident[:, :])
                ins.then_inc(pt_psum, 1)

            def weights_times_v(n, s, par):
                pp, r = (s // 4) % 2, s % 4
                for pl in range(2):
                    for jj in range(2):
                        for hl in range(2):
                            q, lo, hi = 2 * jj + hl, hl * HALF, (hl + 1) * HALF
                            ins = pe.matmul(pOT[32 * q:32 * q + 32, pl * P:(pl + 1) * P],
                                            v1[lo:hi, par, 2 * pp + pl, 2 * r + jj, :, :].rearrange("p b d -> p (b d)"),
                                            pt_sb[lo:hi, s % 2, (pl * 2 + jj) * P:(pl * 2 + jj + 1) * P],
                                            start=True, stop=True)
                ins.then_inc(pv_psum, 1)

            def turn_outputs(n, s, pp):
                r = s % 4
                pe.wait_ge(po_ready, n + 1)
                if r == 0:
                    reach(pe, o_used, pp)
                for pl in range(2):
                    ins = pe.transpose(pO[:, pl, r * P:(r + 1) * P], ot_sb[:, s % 2, pl * P:(pl + 1) * P],
                                       ident[:, :])
                ins.then_inc(o_psum, 1)

            def turn_o(g, par):
                pe.wait_ge(o_used, 2 * g + 2)
                pe.wait_ge(q_ready, at_most(g + 3))
                if isinstance(g, int) and g == GROUPS - 1:
                    pe.wait_ge(ot_ready, g)
                for t in range(TILES):
                    ins = pe.transpose(pM[:, 0, t * P:(t + 1) * P], on[:, par, t, :], ident[:, :])
                ins.then_inc(ot_psum, 1)

            def project_o(g):
                pe.wait_ge(ot_ready, g + 1)
                pe.wait_ge(v_ready, at_most(g + 3))
                if isinstance(g, int) and g == GROUPS - 1:
                    pe.wait_ge(y_done, g)
                for t in range(TILES):
                    ins = pe.matmul(pM[:, 1, t * P:(t + 1) * P], oT[:, t * P:(t + 1) * P], wo[:, :],
                                    start=True, stop=True)
                ins.then_inc(y_psum, 1)

            turn_x(0)
            project_k(0)
            project_q(0)
            project_v(0)
            pe.wait_ge(q_ready, 1)
            pe.wait_ge(v_ready, 1)

            def step(i, first, last):
                for s in range(SLOTS):
                    half, u = s // UNITS, s % UNITS
                    c = 2 * i + half
                    n = i * SLOTS + s
                    if u == 0:
                        pe.wait_ge(q_ready, c + 1)
                    scores(n, s, half)
                    if not (first and s < 2):
                        turn_weights(n - 2, (s - 2) % 16)
                    if not (first and s < 3):
                        q = (s - 3) % 16
                        if u == 3:
                            pe.wait_ge(v_ready, c + 1)
                        pe.wait_ge(pt_ready, n - 2)
                        if not (first and s < 4):
                            turn_outputs(n - 4, (s - 4) % 16, 4 * i + (s - 4) // 4)
                        weights_times_v(n - 3, q, q // UNITS)
                    if not (last and half == 1):
                        if u == 0:
                            turn_x(c + 1)
                        if u == 2:
                            project_k(c + 1)
                        if u == 3:
                            project_q(c + 1)
                        if u == 4:
                            project_v(c + 1)
                    if u == 5 and not (first and half == 0):
                        turn_o(c - 1, 1 - half)
                    if u == 6 and not (first and half == 0) and not guarded:
                        project_o(c - 1)
            two_groups(pe, step)
            N = GROUPS * UNITS
            turn_weights(N - 2, 14)
            pe.wait_ge(pt_ready, N - 2)
            turn_outputs(N - 4, 12, 15)
            weights_times_v(N - 3, 13, 1)
            turn_weights(N - 1, 15)
            pe.wait_ge(pt_ready, N - 1)
            turn_outputs(N - 3, 13, 15)
            weights_times_v(N - 2, 14, 1)
            pe.wait_ge(pt_ready, N)
            turn_outputs(N - 2, 14, 15)
            weights_times_v(N - 1, 15, 1)
            turn_outputs(N - 1, 15, 15)
            turn_o(GROUPS - 1, 1)
            if not guarded:
                project_o(GROUPS - 1)
            else:
                pe.wait_ge(guard, 3 + GROUPS)
                pe.wait_ge(o_used, 16)
                pe.matmul(pO[:, 0, 0:1], ones[:, :], nan_col[:, 0:1], start=True, stop=True)
                pe.matmul(pO[:, 1, 0:BATCH], wv_all[:, :], kv_mean[:, :], start=True, stop=True).then_inc(flag_psum, 1)
                pe.wait_ge(guard, 6 + GROUPS)
                for g in range(GROUPS):
                    reach(pe, y_done, g - 1)
                    for t in range(TILES):
                        t0 = g * GROUP + t * P
                        ins = pe.matmul(pM[:, g % 2, t * P:(t + 1) * P], oT[:, t0:t0 + P], wo[:, :],
                                        start=True, stop=True)
                    ins.then_inc(y_psum, 1)


def mamba_phase(nc, pre, w, src, dst):
    N = 16
    RANK = 8
    TAPS = 4
    PAD = TAPS - 1
    SEQS = GROUP // SEQ
    SLOTS = 2 * N
    STEPS = GROUPS // 2
    XD = 2 * N + RANK
    with ExitStack() as ctx:
        m = Memory(nc, ctx, pre)
        ctx.callback(m.clear)
        ident = m.sb("ident", [P, P])
        w_in_t = m.sb("w_in_t", [D, 4, P])
        conv_w = m.sb("conv_w", [P, TAPS, 2, P])
        w_taps = m.sb("w_taps", [D, TAPS, 2, P])
        conv_b = m.sb("conv_b", [P, 2])
        w_x = m.sb("w_x", [P, 2, XD])
        w_dt = m.sb("w_dt", [RANK, 2, P])
        b_dt = m.sb("b_dt", [P, 2])
        a_neg = m.sb("a_neg", [P, 2, N])
        d_skip = m.sb("d_skip", [P, 2])
        w_out_t = m.sb("w_out_t", [P, 2, D])
        sel = m.sb("sel", [3 * 2 * N, 2 * N])
        sel_bf = m.sb("sel_bf", [3 * 2 * N, 2 * N, P], BF16)
        x = m.sb("x", [P, GROUPS * TILES, D])
        ln = LayerNorm(m)
        xn = m.sb("xn", [P, TILES, D])
        xnT = m.sb("xnT", [D, SEQS, PAD + SEQ])
        z = m.sb("z", [P, 2, GROUP])
        z_gate = m.sb("z_gate", [P, 2, 2, GROUP])
        xs = m.sb("xs", [P, 2, 2, GROUP])
        dt_low = m.sb("dt_low", [RANK, GROUP])
        rest = m.sb("rest", [P, GROUP])
        split = m.sb("split", [3 * 2 * N, 2, GROUP], BF16)
        absv = m.sb("absv", [P, 2, GROUP])
        e1 = m.sb("e1", [P, 2, GROUP])
        e1p = m.sb("e1p", [P, 2, GROUP])
        lnv = m.sb("lnv", [P, 2, GROUP])
        relu = m.sb("relu", [P, 2, GROUP])
        dt = m.sb("dt", [P, 2, 2, GROUP])
        u = m.sb("u", [P, 2, 2, GROUP])
        dA = m.sb("dA", [P, 4, 2, SEQS, SEQ])
        b_sb = m.sb("b_sb", [P, 4, GROUP])
        dbx = m.sb("dbx", [P, 4, 2, GROUP])
        h = m.sb("h", [P, 2, 2, GROUP])
        hc = m.sb("hc", [P, 4, 2, GROUP])
        y_skip = m.sb("y_skip", [P, 2, GROUP])
        y_gated = m.sb("y_gated", [P, 2, GROUP])

        pB = m.ps("pB", [P, 2, GROUP])
        pC = m.ps("pC", [P, 2, GROUP])
        pY = m.ps("pY", [P, 2, GROUP])
        pM = m.ps("pM", [P, 2, GROUP])

        (w_in, x_first, x_rest, consts, chain, setup, a_exp) = [
            m.sem(k) for k in ("w_in", "x_first", "x_rest", "consts", "chain", "setup", "a_exp")]
        var_ready, rstd_ready, xn_ready = m.sem("var_ready"), m.sem("rstd_ready"), m.sem("xn_ready")
        xT_psum, xnT_ready, z_psum, z_ready = m.sem("xT_psum"), m.sem("xnT_ready"), m.sem("z_psum"), m.sem("z_ready")
        xs_psum, zg_ready, xs_ready = m.sem("xs_psum"), m.sem("zg_ready"), m.sem("xs_ready")
        xd_psum, hi_ready, low_ready = m.sem("xd_psum"), m.sem("hi_ready"), m.sem("low_ready")
        rest_ready, mid_ready, split_ready = m.sem("rest_ready"), m.sem("mid_ready"), m.sem("split_ready")
        dt_psum, soft_link, ln_ready, relu_ready = m.sem("dt_psum"), m.sem("soft_link"), m.sem("ln_ready"), m.sem("relu_ready")
        err_ready, fix_ready, dt_ready, u_ready = m.sem("err_ready"), m.sem("fix_ready"), m.sem("dt_ready"), m.sem("u_ready")
        da_ready, b_psum, b_ready, dbx_ready = m.sem("da_ready"), m.sem("b_psum"), m.sem("b_ready"), m.sem("dbx_ready")
        scan_done, c_psum, hc_ready, y_psum = m.sem("scan_done"), m.sem("c_psum"), m.sem("hc_ready"), m.sem("y_psum")
        y_used, y_ready, o_psum, o_done, x_out = m.sem("y_used"), m.sem("y_ready"), m.sem("o_psum"), m.sem("o_done"), m.sem("x_out")

        block = ctx.enter_context(nc.Block())
        NW = 11

        def two_groups(eng, step):
            step(0, True, False)
            with eng.Fori(1, STEPS - 1) as i:
                step(i, False, False)
            step(STEPS - 1, False, True)

        def xg(g):
            return x[:, bass.ds(g * TILES, TILES), :]

        @block.sync
        def _(sp):
            def load(g, n, sem):
                sp.dma_start(x[:, g * TILES:(g + n) * TILES, :],
                             src.rearrange("(n p) d -> p n d", p=P)[:, g * TILES:(g + n) * TILES, :]
                             ).then_inc(sem, 16)

            load(0, 1, x_first)
            for buf, name in ((ident, "ident"), (w_in_t, "w_in_t"), (conv_b, "conv_b"), (w_x, "w_x"),
                              (w_dt, "w_dt"), (b_dt, "b_dt"), (a_neg, "a_log"), (d_skip, "d_skip"),
                              (w_out_t, "w_out_t"), (sel, "sel")):
                sp.dma_start(everything(buf), w[name if name == "ident" else f"{pre}_{name}"]).then_inc(w_in, 16)
            sp.dma_start(conv_w[:, :, :, :], w[pre + "_conv_w"].partition_broadcast(P)).then_inc(w_in, 16)
            load(1, GROUPS - 1, x_rest)
            sp.wait_ge(x_first, 16)
            sp.wait_ge(x_rest, 16)
            with sp.Fori(0, GROUPS) as g:
                sp.wait_ge(o_done, g + 1)
                sp.dma_start(rows(dst, g), xg(g)).then_inc(x_out, 16)
            sp.wait_ge(x_out, 16 * GROUPS)

        @block.gpsimd
        def _(pool):
            pool.memset(ln.minus_half[:, :], -0.5).then_inc(consts, 1)
            pool.memset(dA[:, :, :, :, 0:1], 0.0).then_inc(consts, 1)
            pool.memset(xnT[:, :, 0:PAD], 0.0).then_inc(consts, 1)
            pool.wait_ge(consts, 3)

            def rstd(g):
                pool.wait_ge(var_ready, g + 1)
                pool.tensor_tensor(ln.rstd[:, :], ln.var_eps[:, :], ln.minus_half[:, :],
                                   ALU.pow).then_inc(rstd_ready, 1)

            def soft_fix(g):
                pool.wait_ge(ln_ready, g + 1)
                pool.wait_ge(err_ready, g + 1)
                pool.tensor_tensor(lnv[:, :, :], lnv[:, :, :], e1[:, :, :], ALU.subtract).then_inc(fix_ready, 1)

            def times_b(k, s):
                pool.wait_ge(b_ready, k + 1)
                reach(pool, scan_done, k - 3)
                pool.tensor_tensor(dbx[:, s % 4, :, :], u[:, s // N, :, :], bc(b_sb[:, s % 4, :], 1, 2),
                                   ALU.mult).then_inc(dbx_ready, 1)

            rstd(0)
            rstd(1)
            soft_fix(0)

            def step(i, first, last):
                for s in range(SLOTS):
                    c, n = 2 * i + s // N, s % N
                    if n == 0:
                        pool.wait_ge(u_ready, c + 1)
                    times_b(i * SLOTS + s, s)
                    if n == 10 and not last:
                        rstd(c + 2)
                    if n == 12 and not (last and s >= N):
                        soft_fix(c + 1)
            two_groups(pool, step)

        @block.vector
        def _(v):
            v.wait_ge(consts, 3)
            v.wait_ge(x_first, 16)

            def layer_norm(g, link):
                if isinstance(g, int) and g == 1:
                    v.wait_ge(x_rest, 16)
                layer_norm_stats(v, link, xg(g), ln)
                v.tensor_tensor(ln.var_eps[:, :], ln.m2[:, :], ln.dm2[:, :], ALU.add).then_inc(var_ready, 1)

            def normalised(g):
                reach(v, xT_psum, g)
                v.wait_ge(rstd_ready, g + 1)
                layer_norm_apply(v, xg(g), ln, xn).then_inc(xn_ready, 1)
                v.wait_ge(xn_ready, g + 1)

            def split_rest(g):
                v.wait_ge(hi_ready, g + 1)
                v.tensor_tensor(rest[32:64, :], pM[0:32, 0, :], split[0:32, g_par(g), :],
                                ALU.subtract).then_inc(rest_ready, 1)

            def split_last(g):
                v.wait_ge(mid_ready, g + 1)
                v.tensor_tensor(split[64:96, g_par(g), :], rest[32:64, :], split[32:64, g_par(g), :],
                                ALU.subtract).then_inc(split_ready, 1)

            def g_par(g):
                return par_of[0]
            par_of = [0]

            def rounding_of_1p(g):
                v.wait_ge(soft_link, 2 * g + 2)
                v.scalar_tensor_tensor(e1[:, :, :], e1p[:, :, :], -1.0, e1[:, :, :], ALU.add,
                                       ALU.subtract).then_inc(err_ready, 1)

            def make_dt(g, par):
                reach(v, da_ready, (g - 1) * N)
                v.wait_ge(fix_ready, g + 1)
                v.wait_ge(relu_ready, g + 1)
                v.tensor_tensor(dt[:, par, :, :], lnv[:, :, :], relu[:, :, :], ALU.add).then_inc(dt_ready, 1)

            def make_u(g, par):
                v.wait_ge(dt_ready, g + 1)
                v.wait_ge(xs_ready, g + 1)
                reach(v, dbx_ready, (g - 1) * N)
                v.tensor_tensor(u[:, par, :, :], dt[:, par, :, :], xs[:, par, :, :], ALU.mult).then_inc(u_ready, 1)

            def scan(k, s):
                v.wait_ge(da_ready, k + 1)
                v.wait_ge(dbx_ready, k + 1)
                reach(v, hc_ready, k - 1)
                v.tensor_tensor_scan(h[:, s % 2, :, :].rearrange("p a t -> p (a t)"),
                                     dA[:, s % 4, :, :, :].rearrange("p a b t -> p (a b t)"),
                                     dbx[:, s % 4, :, :].rearrange("p a t -> p (a t)"),
                                     0.0, ALU.mult, ALU.add).then_inc(scan_done, 1)

            def times_c(k, s):
                v.wait_ge(scan_done, k + 1)
                v.wait_ge(c_psum, k + 1)
                reach(v, y_psum, k - 3)
                v.tensor_tensor(hc[:, s % 4, :, :], h[:, s % 2, :, :], bc(pC[:, s % 2, :], 1, 2),
                                ALU.mult).then_inc(hc_ready, 1)

            def skip(g, par):
                v.wait_ge(y_psum, (g + 1) * N)
                reach(v, y_ready, g)
                for half in range(2):
                    ins = v.scalar_tensor_tensor(y_skip[:, half, :], xs[:, par, half, :], d_skip[:, half:half + 1],
                                                 pY[:, half, :], ALU.mult, ALU.add)
                ins.then_inc(y_used, 1)

            def gate(g, par):
                v.wait_ge(y_used, g + 1)
                reach(v, o_psum, g)
                v.tensor_tensor(y_gated[:, :, :], y_skip[:, :, :], z_gate[:, par, :, :], ALU.mult).then_inc(y_ready, 1)

            def residual(g):
                v.wait_ge(o_psum, g + 1)
                v.tensor_tensor(xg(g), pM[:, 1, :].rearrange("p (t d) -> p t d", d=D), xg(g),
                                ALU.add).then_inc(o_done, 1)

            link = linker(v, Count(chain, 0))
            layer_norm(0, link)
            normalised(0)
            v.wait_ge(w_in, 16 * NW)
            v.tensor_tensor(w_taps[:, :, :, :], conv_w[:, :, :, :], bc(w_in_t[:, 0:2, :], 1, TAPS), ALU.mult)
            v.tensor_copy(sel_bf[:, :, :], bc(sel[:, :], 2, P))
            v.wait_ge(a_exp, 1)
            v.tensor_scalar(a_neg[:, :, :], a_neg[:, :, :], -1.0, None, ALU.mult).then_inc(setup, 1)
            layer_norm(1, link)
            normalised(1)
            split_rest(0)
            split_last(0)
            rounding_of_1p(0)
            make_dt(0, 0)
            make_u(0, 0)

            def step(i, first, last):
                for s in range(SLOTS):
                    half, n = s // N, s % N
                    c = 2 * i + half
                    k = i * SLOTS + s
                    scan(k, s)
                    if not (first and s == 0):
                        times_c(k - 1, (s - 1) % SLOTS)
                    if not (first and half == 0):
                        if n == 2:
                            skip(c - 1, 1 - half)
                        if n == 3:
                            gate(c - 1, 1 - half)
                        if n == 5:
                            residual(c - 1)
                    if not (last and half == 1):
                        par_of[0] = 1 - half
                        if n == 9:
                            split_rest(c + 1)
                        if n == 11:
                            split_last(c + 1)
                        if n == 12:
                            rounding_of_1p(c + 1)
                        if n == 13:
                            make_dt(c + 1, 1 - half)
                        if n == 14:
                            make_u(c + 1, 1 - half)
                    if not last:
                        if n == 10:
                            link = linker(v, Count(chain, (c + 2) * ln.LINKS))
                            layer_norm(c + 2, link)
                        if n == 12:
                            normalised(c + 2)
            two_groups(v, step)
            times_c(GROUPS * N - 1, SLOTS - 1)
            skip(GROUPS - 1, 1)
            gate(GROUPS - 1, 1)
            residual(GROUPS - 1)

        @block.scalar
        def _(act):
            act.wait_ge(w_in, 16 * NW)
            act.activation(a_neg[:, :, :], a_neg[:, :, :], ACT.Exp).then_inc(a_exp, 1)
            act.wait_ge(setup, 1)
            act.wait_ge(consts, 3)

            def copy_xT(g):
                reach(act, xs_psum, 2 * g)
                act.wait_ge(xT_psum, g + 1)
                act.activation(xnT[:, :, PAD:PAD + SEQ], pM[:, 0, :].rearrange("p (b t) -> p b t", t=SEQ),
                               ACT.Identity).then_inc(xnT_ready, 1)

            def copy_z(g, half):
                reach(act, zg_ready, g)
                act.wait_ge(z_psum, 2 * g + half + 1)
                act.activation(z[:, half, :], pM[:, 1 - half, :], ACT.Identity).then_inc(z_ready, 1)

            def silu(g, par):
                act.wait_ge(z_ready, 2 * g + 2)
                reach(act, y_ready, g - 1)
                act.activation(z_gate[:, par, :, :], z[:, :, :], ACT.Silu).then_inc(zg_ready, 1)
                reach(act, y_used, g - 1)
                for half in range(2):
                    act.wait_ge(xs_psum, 2 * g + half + 1)
                    ins = act.activation(xs[:, par, half, :], pM[:, half, :], ACT.Silu, bias=conv_b[:, half:half + 1])
                ins.then_inc(xs_ready, 1)

            def split_first(g, par):
                act.wait_ge(xd_psum, g + 1)
                reach(act, c_psum, (g - 1) * N)
                act.activation(split[0:32, par, :], pM[0:32, 0, :], ACT.Identity).then_inc(hi_ready, 1)
                reach(act, dt_psum, 2 * g)
                act.activation(dt_low[:, :], pM[32:32 + RANK, 0, :], ACT.Identity).then_inc(low_ready, 1)

            def split_second(g, par):
                act.wait_ge(rest_ready, g + 1)
                act.activation(split[32:64, par, :], rest[32:64, :], ACT.Identity).then_inc(mid_ready, 1)

            def softplus(g):
                reach(act, dt_ready, g)
                act.wait_ge(dt_psum, 2 * g + 2)
                for half in range(2):
                    act.activation(absv[:, half, :], pM[:, 1 - half, :], ACT.Abs, bias=b_dt[:, half:half + 1])
                    ins = act.activation(relu[:, half, :], pM[:, 1 - half, :], ACT.Relu, bias=b_dt[:, half:half + 1])
                ins.then_inc(relu_ready, 1)
                act.wait_ge(relu_ready, g + 1)
                act.activation(e1[:, :, :], absv[:, :, :], ACT.Exp, scale=-1.0).then_inc(soft_link, 1)
                act.wait_ge(soft_link, 2 * g + 1)
                act.activation(e1p[:, :, :], e1[:, :, :], ACT.Identity, bias=1.0).then_inc(soft_link, 1)

            def logarithm(g):
                act.wait_ge(soft_link, 2 * g + 2)
                act.activation(lnv[:, :, :], e1p[:, :, :], ACT.Ln).then_inc(ln_ready, 1)

            def decay(k, s):
                reach(act, scan_done, k - 3)
                for half in range(2):
                    ins = act.activation(dA[:, s % 4, half, :, 1:SEQ],
                                         dt[:, s // N, half, :].rearrange("p (b t) -> p b t", t=SEQ)[:, :, 1:SEQ],
                                         ACT.Exp, scale=a_neg[:, half, s % N:s % N + 1])
                ins.then_inc(da_ready, 1)

            def copy_b(k, s):
                act.wait_ge(b_psum, k + 1)
                reach(act, dbx_ready, k - 3)
                act.activation(b_sb[:, s % 4, :], pB[:, s % 2, :], ACT.Identity).then_inc(b_ready, 1)

            copy_xT(0)
            copy_z(0, 0)
            copy_z(0, 1)
            silu(0, 0)
            split_first(0, 0)
            split_second(0, 0)
            softplus(0)
            logarithm(0)

            def step(i, first, last):
                for s in range(SLOTS):
                    half, n = s // N, s % N
                    c = 2 * i + half
                    k = i * SLOTS + s
                    if n == 0:
                        act.wait_ge(dt_ready, c + 1)
                    decay(k, s)
                    copy_b(k, s)
                    if not (last and half == 1):
                        if n == 0:
                            copy_xT(c + 1)
                        if n == 1:
                            copy_z(c + 1, 0)
                        if n == 2:
                            copy_z(c + 1, 1)
                        if n == 7:
                            silu(c + 1, 1 - half)
                        if n == 9:
                            split_first(c + 1, 1 - half)
                        if n == 10:
                            split_second(c + 1, 1 - half)
                        if n == 11:
                            softplus(c + 1)
                        if n == 12:
                            logarithm(c + 1)
            two_groups(act, step)

        @block.tensor
        def _(pe):
            pe.wait_ge(setup, 1)

            def turn_x(g):
                pe.wait_ge(xn_ready, g + 1)
                reach(pe, relu_ready, g)
                for t in range(TILES):
                    ins = pe.transpose(pM[:, 0, t * P:(t + 1) * P], xn[:, t, :], ident[:, :])
                ins.then_inc(xT_psum, 1)

            def project_z(g, half):
                pe.wait_ge(xnT_ready, g + 1)
                if half == 0:
                    reach(pe, o_done, g - 2)
                    reach(pe, relu_ready, g)
                pe.matmul(pM[:, 1 - half, :].rearrange("p (b t) -> p b t", t=SEQ), w_in_t[:, 2 + half, :],
                          xnT[:, :, PAD:PAD + SEQ], start=True, stop=True).then_inc(z_psum, 1)

            def project_x(g, half):
                if half == 0:
                    pe.wait_ge(z_ready, 2 * g + 2)
                else:
                    reach(pe, o_done, g - 1)
                for tap in range(TAPS):
                    ins = pe.matmul(pM[:, half, :].rearrange("p (b t) -> p b t", t=SEQ), w_taps[:, tap, half, :],
                                    xnT[:, :, tap:tap + SEQ], start=(tap == 0), stop=(tap == TAPS - 1))
                ins.then_inc(xs_psum, 1)

            def project_bcdt(g, par):
                pe.wait_ge(xs_ready, g + 1)
                for half in range(2):
                    ins = pe.matmul(pM[0:XD, 0, :], w_x[:, half, :], xs[:, par, half, :], start=(half == 0),
                                    stop=(half == 1))
                ins.then_inc(xd_psum, 1)

            def project_dt(g):
                pe.wait_ge(low_ready, g + 1)
                pe.matmul(pM[:, 1, :], w_dt[:, 0, :], dt_low[:, :], start=True, stop=True).then_inc(dt_psum, 1)
                pe.wait_ge(rest_ready, g + 1)
                pe.matmul(pM[:, 0, :], w_dt[:, 1, :], dt_low[:, :], start=True, stop=True).then_inc(dt_psum, 1)

            def send_b(k, s):
                reach(pe, b_ready, k - 1)
                pe.matmul(pB[:, s % 2, :], sel_bf[:, s % N, :], split[:, s // N, :], start=True,
                          stop=True).then_inc(b_psum, 1)

            def send_c(k, s):
                reach(pe, hc_ready, k - 1)
                pe.matmul(pC[:, s % 2, :], sel_bf[:, N + s % N, :], split[:, s // N, :], start=True,
                          stop=True).then_inc(c_psum, 1)

            def add_state(k, s, g):
                pe.wait_ge(hc_ready, k + 1)
                if s % N == 0:
                    reach(pe, y_used, g)
                for half in range(2):
                    ins = pe.matmul(pY[:, half, :], ident[:, :], hc[:, s % 4, half, :], start=(s % N == 0),
                                    stop=(s % N == N - 1))
                ins.then_inc(y_psum, 1)

            def project_out(g):
                pe.wait_ge(y_ready, g + 1)
                if isinstance(g, int) and g == GROUPS - 1:
                    pe.wait_ge(o_done, g)
                else:
                    pe.wait_ge(z_ready, 2 * g + 3)
                for t in range(TILES):
                    for half in range(2):
                        ins = pe.matmul(pM[:, 1, t * P:(t + 1) * P], y_gated[:, half, t * P:(t + 1) * P],
                                        w_out_t[:, half, :], start=(half == 0), stop=(half == 1))
                ins.then_inc(o_psum, 1)

            turn_x(0)
            project_z(0, 0)
            project_z(0, 1)
            project_x(0, 0)
            project_x(0, 1)
            project_bcdt(0, 0)
            project_dt(0)

            def step(i, first, last):
                for s in range(SLOTS):
                    half, n = s // N, s % N
                    c = 2 * i + half
                    k = i * SLOTS + s
                    if n == 0:
                        pe.wait_ge(split_ready, c + 1)
                    send_b(k, s)
                    if not (first and s < 1):
                        send_c(k - 1, (s - 1) % SLOTS)
                    if not (first and s < 3):
                        add_state(k - 3, (s - 3) % SLOTS, c if n >= 3 else c - 1)
                    if not (last and half == 1):
                        if n == 0:
                            turn_x(c + 1)
                        if n == 1:
                            project_z(c + 1, 0)
                        if n == 2:
                            project_z(c + 1, 1)
                        if n == 3:
                            project_x(c + 1, 0)
                        if n == 6:
                            project_x(c + 1, 1)
                        if n == 8:
                            project_bcdt(c + 1, 1 - half)
                        if n == 10:
                            project_dt(c + 1)
                    if n == 4 and not (first and half == 0):
                        project_out(c - 1)
            two_groups(pe, step)
            K = GROUPS * N
            send_c(K - 1, SLOTS - 1)
            for k in range(K - 3, K):
                add_state(k, k % SLOTS, GROUPS - 1)
            project_out(GROUPS - 1)


def ffn_phase(nc, pre, w, src, dst, gated):
    HC = 2 if gated else 4
    MM = 4
    with ExitStack() as ctx:
        m = Memory(nc, ctx, pre)
        ctx.callback(m.clear)
        w1 = m.sb("w1", [P, EXPERTS, MM, P])
        w2 = m.sb("w2", [P, EXPERTS, HC, D])
        b1 = m.sb("b1", [P, EXPERTS, MM])
        b2 = m.sb("b2", [P, EXPERTS, D])
        wr = m.sb("wr", [D, EXPERTS])
        ident = m.sb("ident", [P, P])
        rev = m.sb("rev", [P, EXPERTS])
        euler = m.sb("euler", [P, TILES * EXPERTS])
        xin = m.sb("xin", [P, TILES, D])
        ln = LayerNorm(m)
        xn = m.sb("xn", [P, TILES, D])
        xnT = m.sb("xnT", [D, GROUP])
        hT = m.sb("hT", [P, 2, HC, GROUP])
        sg = m.sb("sg", [P, 2, HC, GROUP]) if gated else None
        acc = m.sb("acc", [P, TILES, D])
        r8 = [m.sb(f"r8_{i}", [P, TILES, EXPERTS]) for i in range(8)]
        lgs, ex, key1, oh1, l2, key2, oh2, comb = r8
        r1 = [m.sb(f"r1_{i}", [P, TILES]) for i in range(8)]
        max1, kmax1, max2, kmax2, ssum, zsum, rsum, _ = r1

        pT = m.ps("pT", [P, GROUP])
        plg = m.ps("plg", [P, GROUP])
        pH = m.ps("pH", [P, 4, GROUP])
        pY = m.ps("pY", [P, 2, TILES, D])

        weights_in = m.sem("weights_in")
        x_in = m.sem("x_in")
        x_out = m.sem("x_out")
        consts = m.sem("consts")
        var_ready = m.sem("var_ready")
        rstd_ready = m.sem("rstd_ready")
        xn_ready = m.sem("xn_ready")
        xT_psum = m.sem("xT_psum")
        xnT_ready = m.sem("xnT_ready")
        lg_ready = m.sem("lg_ready")
        lgs_ready = m.sem("lgs_ready")
        ex_ready = m.sem("ex_ready")
        comb_ready = m.sem("comb_ready")
        h_psum = m.sem("h_psum")
        act_done = m.sem("act_done")
        gated_done = m.sem("gated_done")
        y_psum = m.sem("y_psum")
        y_used = m.sem("y_used")
        acc_ready = m.sem("acc_ready")
        chain = m.sem("chain")

        block = ctx.enter_context(nc.Block())
        func = ACT.Silu if gated else ACT.Gelu_apprx_tanh
        NW = 7
        ACTS = HC if gated else MM
        LAST = GROUPS - 1
        E = EXPERTS

        def each_group(eng, step):
            step(0, True, False)
            with eng.Fori(1, LAST) as g:
                step(g, False, False)
            step(LAST, False, True)

        @block.sync
        def _(sp):
            sp.dma_start(xin[:, :, :], rows(src, 0)).then_inc(x_in, 16)
            for buf, name in ((ident, "ident"), (wr, pre + "_wr"), (w1, pre + "_w1"), (b1, pre + "_b1"),
                              (w2, pre + "_w2"), (rev, "rev")):
                sp.dma_start(buf[tuple(slice(None) for _ in buf.shape)], w[name]).then_inc(weights_in, 16)
            sp.dma_start(b2[:, :, :], w[pre + "_b2"].partition_broadcast(P)).then_inc(weights_in, 16)

            def step(g, first, last):
                if not last:
                    sp.wait_ge(acc_ready, g * E + 1)
                    sp.dma_start(xin[:, :, :], rows(src, g + 1)).then_inc(x_in, 16)
                sp.wait_ge(acc_ready, g * E + E)
                sp.dma_start(rows(dst, g), acc[:, :, :]).then_inc(x_out, 16)
            each_group(sp, step)
            sp.wait_ge(x_out, 16 * GROUPS)

        @block.gpsimd
        def _(pool):
            pool.memset(euler[:, :], float(np.e)).then_inc(consts, 1)
            pool.memset(ln.minus_half[:, :], -0.5).then_inc(consts, 1)
            pool.wait_ge(consts, 2)
            pool.wait_ge(var_ready, 1)
            pool.tensor_tensor(ln.rstd[:, :], ln.var_eps[:, :], ln.minus_half[:, :], ALU.pow).then_inc(rstd_ready, 1)

            def step(g, first, last):
                pool.wait_ge(lgs_ready, g + 1)
                pool.tensor_tensor(ex[:, :, :].rearrange("p t e -> p (t e)"), euler[:, :],
                                   lgs[:, :, :].rearrange("p t e -> p (t e)"), ALU.pow).then_inc(ex_ready, 1)
                if not last:
                    pool.wait_ge(var_ready, g + 2)
                    pool.tensor_tensor(ln.rstd[:, :], ln.var_eps[:, :], ln.minus_half[:, :],
                                       ALU.pow).then_inc(rstd_ready, 1)
            each_group(pool, step)

        @block.vector
        def _(v):
            LN_LINKS = ln.LINKS
            PER_GROUP = LN_LINKS + (15 if gated else 14)
            v.wait_ge(weights_in, 16 * NW)

            def layer_norm(g, link):
                v.wait_ge(x_in, g * 16 + 16)
                layer_norm_stats(v, link, xin, ln)
                v.tensor_tensor(ln.var_eps[:, :], ln.m2[:, :], ln.dm2[:, :], ALU.add).then_inc(var_ready, 1)
                v.wait_ge(rstd_ready, g + 1)
                layer_norm_apply(v, xin, ln, xn).then_inc(xn_ready, 1)

            def router(g, link):
                v.wait_ge(lg_ready, g + 1)
                lg = plg[:, 0:TILES * E].rearrange("p (t e) -> p t e", e=E)
                link(v.tensor_reduce(max1[:, :], lg, AX.X, ALU.max))
                v.tensor_tensor(lgs[:, :, :], lg, bc(max1[:, :], 2, E), ALU.subtract).then_inc(lgs_ready, 1)
                v.wait_ge(lgs_ready, g + 1)
                revt = bc(rev[:, :], 1, TILES)
                link(v.scalar_tensor_tensor(key1[:, :, :], lgs[:, :, :], 0.0, revt, ALU.is_ge, ALU.mult))
                link(v.tensor_reduce(kmax1[:, :], key1[:, :, :], AX.X, ALU.max))
                link(v.tensor_tensor(oh1[:, :, :], key1[:, :, :], bc(kmax1[:, :], 2, E), ALU.is_equal))
                link(v.scalar_tensor_tensor(l2[:, :, :], oh1[:, :, :], -3e38, lgs[:, :, :], ALU.mult, ALU.add))
                link(v.tensor_reduce(max2[:, :], l2[:, :, :], AX.X, ALU.max))
                link(v.tensor_tensor(key2[:, :, :], l2[:, :, :], bc(max2[:, :], 2, E), ALU.is_equal))
                link(v.tensor_tensor(key2[:, :, :], key2[:, :, :], revt, ALU.mult))
                link(v.tensor_reduce(kmax2[:, :], key2[:, :, :], AX.X, ALU.max))
                link(v.tensor_tensor(oh2[:, :, :], key2[:, :, :], bc(kmax2[:, :], 2, E), ALU.is_equal))
                link(v.tensor_tensor(oh2[:, :, :], oh2[:, :, :], oh1[:, :, :], ALU.add))
                v.wait_ge(ex_ready, g + 1)
                link(v.tensor_tensor(comb[:, :, :], ex[:, :, :], oh2[:, :, :], ALU.mult))
                if gated:
                    v.tensor_reduce(zsum[:, :], ex[:, :, :], AX.X, ALU.add)
                link(v.tensor_reduce(ssum[:, :], comb[:, :, :], AX.X, ALU.add))
                if gated:
                    link(v.scalar_tensor_tensor(ssum[:, :], zsum[:, :], 1e-9, ssum[:, :], ALU.mult, ALU.add))
                link(v.reciprocal(rsum[:, :], ssum[:, :]))
                v.tensor_tensor(comb[:, :, :], comb[:, :, :], bc(rsum[:, :], 2, E), ALU.mult).then_inc(comb_ready, 1)
                v.wait_ge(comb_ready, g + 1)

            def gate_up(g, e):
                for c in range(HC):
                    v.wait_ge(act_done, g * (E * ACTS) + e * ACTS + c + 1)
                    v.wait_ge(h_psum, g * (E * MM) + e * MM + HC + c + 1)
                    v.scalar_tensor_tensor(hT[:, e % 2, c, :], pH[:, HC + c, :], b1[:, e, HC + c:HC + c + 1],
                                           sg[:, e % 2, c, :], ALU.add, ALU.mult).then_inc(gated_done, 1)

            def sum_expert(g, first, e, link):
                if e == 0 and not first:
                    v.wait_ge(x_out, g * 16)
                v.wait_ge(y_psum, g * E + e + 1)
                base = xin if e == 0 else acc
                for t in range(TILES):
                    ins = v.scalar_tensor_tensor(acc[:, t, :], pY[:, e % 2, t, :], comb[:, t, e:e + 1],
                                                 base[:, t, :], ALU.mult, ALU.add)
                ins.then_inc(y_used, 1)
                v.wait_ge(y_used, g * E + e + 1)
                for t in range(TILES):
                    ins = v.scalar_tensor_tensor(acc[:, t, :], b2[:, e, :], comb[:, t, e:e + 1],
                                                 acc[:, t, :], ALU.mult, ALU.add)
                ins.then_inc(acc_ready, 1)
                v.wait_ge(acc_ready, g * E + e + 1)

            count = Count(chain, 0)
            layer_norm(0, linker(v, count))
            assert count.n == LN_LINKS

            def step(g, first, last):
                count = Count(chain, g * PER_GROUP + LN_LINKS)
                link = linker(v, count)
                router(g, link)
                if gated:
                    gate_up(g, 0)
                for e in range(E):
                    if gated and e + 1 < E:
                        gate_up(g, e + 1)
                    sum_expert(g, first, e, link)
                    if e == E - 3 and not last:
                        layer_norm(g + 1, link)
                assert last or count.n == PER_GROUP, count.n

            each_group(v, step)

        @block.scalar
        def _(act):
            act.wait_ge(weights_in, 16 * NW)

            def copy_xT(g):
                act.wait_ge(xT_psum, g + 1)
                act.activation(xnT[:, :], pT[:, :], ACT.Identity).then_inc(xnT_ready, 1)

            copy_xT(0)

            def step(g, first, last):
                for e in range(E):
                    for c in range(ACTS):
                        act.wait_ge(h_psum, g * (E * MM) + e * MM + c + 1)
                        if c == 0 and not (first and e < 2):
                            act.wait_ge(y_psum, g * E + e - 1)
                        out = sg if gated else hT
                        act.activation(out[:, e % 2, c, :], pH[:, c, :], func,
                                       bias=b1[:, e, c:c + 1]).then_inc(act_done, 1)
                if not last:
                    copy_xT(g + 1)
            each_group(act, step)

        @block.tensor
        def _(pe):
            pe.wait_ge(weights_in, 16 * NW)

            def transposes(g):
                pe.wait_ge(xn_ready, g + 1)
                for t in range(TILES):
                    ins = pe.transpose(pT[:, t * P:(t + 1) * P], xn[:, t, :], ident[:, :])
                ins.then_inc(xT_psum, 1)

            def router(g):
                pe.wait_ge(xnT_ready, g + 1)
                for t in range(TILES):
                    ins = pe.matmul(plg[:, t * E:(t + 1) * E], xnT[:, t * P:(t + 1) * P], wr[:, :],
                                    start=True, stop=True)
                ins.then_inc(lg_ready, 1)

            def hidden(g, first, e):
                for c in range(MM):
                    if not (first and e == 0):
                        if c < ACTS:
                            pe.wait_ge(act_done, g * (E * ACTS) + (e - 1) * ACTS + c + 1)
                        else:
                            pe.wait_ge(gated_done, g * (E * HC) + (e - 1) * HC + c - HC + 1)
                    pe.matmul(pH[:, c, :], w1[:, e, c, :], xnT[:, :], start=True, stop=True).then_inc(h_psum, 1)

            def output(g, first, e):
                if gated:
                    pe.wait_ge(gated_done, g * (E * HC) + (e + 1) * HC)
                else:
                    pe.wait_ge(act_done, g * (E * ACTS) + (e + 1) * ACTS)
                if not (first and e < 2):
                    pe.wait_ge(y_used, g * E + e - 1)
                for t in range(TILES):
                    for c in range(HC):
                        ins = pe.matmul(pY[:, e % 2, t, :], hT[:, e % 2, c, t * P:(t + 1) * P], w2[:, e, c, :],
                                        start=(c == 0), stop=(c == HC - 1))
                ins.then_inc(y_psum, 1)

            transposes(0)

            def step(g, first, last):
                router(g)
                hidden(g, first, 0)
                for e in range(E):
                    if e + 1 < E:
                        hidden(g, first, e + 1)
                    elif not last:
                        transposes(g + 1)
                    output(g, first, e)
            each_group(pe, step)


def decoder_program(nc, w, y):
    between = [nc.dram_tensor(f"x_{i}", (TOKENS, D), F32).ap() for i in range(5)]
    mamba_phase(nc, "M", w, w["x"], between[0])
    attention_phase(nc, "X0", w, between[0], between[1], w["ctxT"], guarded=True)
    ffn_phase(nc, "F0", w, between[1], between[2], gated=False)
    attention_phase(nc, "S1", w, between[2], between[3], None, self_attn=True)
    attention_phase(nc, "X1", w, between[3], between[4], w["ctxT"])
    ffn_phase(nc, "F1", w, between[4], y, gated=True)


def layouts(i):
    f = {
        "x": i["x"].reshape(TOKENS, D),
        "ctxT": i["ctx_768"].reshape(TOKENS, DC).T,
        "ident": np.eye(P, dtype=np.float32),
        "mask": (np.arange(P)[:, None] // HD % 4 == np.arange(4)[None]).astype(np.float32),
        "rev": np.broadcast_to(np.arange(EXPERTS, 0, -1, dtype=np.float32), (P, EXPERTS)),
        "M_sel": (np.arange(96)[:, None] % 32 == np.arange(32)[None]).astype(np.float32),
    }
    n = "L0_attn_"
    f["M_w_in_t"] = i[n + "W_in"].T.reshape(D, 4, P)
    f["M_conv_w"] = i[n + "conv_w"].reshape(2, P, 4).transpose(2, 0, 1)
    f["M_conv_b"] = i[n + "conv_b"].reshape(2, P).T
    f["M_w_x"] = np.roll(i[n + "W_x"].T, -8, axis=1).reshape(2, P, 40).transpose(1, 0, 2)
    f["M_w_dt"] = i[n + "W_dt"].T.reshape(8, 2, P)
    f["M_b_dt"] = i[n + "b_dt"].reshape(2, P).T
    f["M_a_log"] = i[n + "A_log"].reshape(2, P, 16).transpose(1, 0, 2)
    f["M_d_skip"] = i[n + "D"].reshape(2, P).T
    f["M_w_out_t"] = i[n + "W_out"].T.reshape(2, P, D).transpose(1, 0, 2)

    def by_parity(a):
        return a.reshape(len(a), HEADS // 2, 2, HD).transpose(0, 2, 1, 3).reshape(len(a), 2, D // 2)

    for pre, n in (("X0", "L0_xattn_"), ("X1", "L1_xattn_")):
        f[pre + "_wq"], f[pre + "_wk"], f[pre + "_wo"] = i[n + "Wq"], i[n + "Wk"], i[n + "Wo"]
        f[pre + "_wv"], f[pre + "_bv"] = by_parity(i[n + "Wv"]), by_parity(i[n + "bv"][None])[0]
        f[pre + "_bq"], f[pre + "_bk"], f[pre + "_bo"] = i[n + "bq"][:, None], i[n + "bk"][:, None], i[n + "bo"]
    f["X0_wv_all"], f["X0_bv_col"] = i["L0_xattn_Wv"], i["L0_xattn_bv"][:, None]
    wt = i["L1_attn_in_proj_weight"].reshape(HEADS, 3, HD, D)
    bt = i["L1_attn_in_proj_bias"].reshape(HEADS, 3, HD)
    f["S1_wq"], f["S1_wk"] = (wt[:, k].reshape(P, D).T for k in range(2))
    f["S1_wv"] = by_parity(wt[:, 2].reshape(P, D).T)
    f["S1_wo"] = i["L1_attn_out_proj_weight"].T
    f["S1_bq"], f["S1_bk"] = (bt[:, k].reshape(P)[:, None] for k in range(2))
    f["S1_bv"], f["S1_bo"] = by_parity(bt[:, 2].reshape(1, P))[0], i["L1_attn_out_proj_bias"]

    f["F0_wr"], f["F0_b2"] = i["L0_ffn_Wg"], i["L0_ffn_b2"]
    f["F0_w1"] = i["L0_ffn_W1"].transpose(1, 0, 2).reshape(D, EXPERTS, 4, P)
    f["F0_w2"] = i["L0_ffn_W2"].reshape(EXPERTS, 4, P, D).transpose(2, 0, 1, 3)
    f["F0_b1"] = i["L0_ffn_b1"].reshape(EXPERTS, 4, P).transpose(2, 0, 1)
    n = "L1_ffn_"
    f["F1_wr"], f["F1_b2"] = i[n + "router_w"].T, i[n + "down_b"]
    f["F1_w1"] = np.concatenate([i[n + k].transpose(1, 0, 2).reshape(D, EXPERTS, 2, P) for k in ("gate_w", "up_w")], 2)
    f["F1_w2"] = i[n + "down_w"].reshape(EXPERTS, 2, P, D).transpose(2, 0, 1, 3)
    f["F1_b1"] = np.concatenate([i[n + k].reshape(EXPERTS, 2, P).transpose(2, 0, 1) for k in ("gate_b", "up_b")], 2)
    return {k: np.ascontiguousarray(a) for k, a in f.items()}


def kernel(**inputs):
    import concourse.bacc as _bacc
    from concourse.bass_utils import run_bass_kernel_spmd as _run

    nc = _bacc.Bacc("TRN2", target_bir_lowering=False, num_devices=1)
    arrays, w = {}, {}
    for name, a in layouts({k: np.asarray(a) for k, a in inputs.items()}).items():
        arrays[f"in_{name}"] = a
        w[name] = nc.dram_tensor(f"in_{name}", a.shape, mybir.dt.from_np(a.dtype), kind="ExternalInput").ap()
    y = nc.dram_tensor("out", (TOKENS, D), F32, kind="ExternalOutput").ap()
    decoder_program(nc, w, y)
    r = _run(nc, [arrays], core_ids=[0])
    return r.results[0]["out"].reshape(BATCH, SEQ, D)
```

```python
import numpy as np
from contextlib import ExitStack

import concourse.bass as bass
from concourse import mybir

BATCH, SEQ, D, DC = 64, 64, 128, 96
TOKENS = BATCH * SEQ
P = 128
GROUP = 512
TILES = GROUP // P
GROUPS = TOKENS // GROUP
EXPERTS = 8
HEADS, HD = 16, 8
LN_EPS = 1e-5

F32 = mybir.dt.float32
BF16 = mybir.dt.bfloat16
I32 = mybir.dt.int32
ALU = mybir.AluOpType
ACT = mybir.ActivationFunctionType
AX = mybir.AxisListType


class Count:

    def __init__(self, sem, base=0):
        self.sem, self.base, self.n = sem, base, 0

    def at(self, n):
        return self.base + n

    def __call__(self, ins):
        ins.then_inc(self.sem, 1)
        self.n += 1
        return ins


def linker(eng, count):
    def link(ins):
        count(ins)
        eng.wait_ge(count.sem, count.at(count.n))
        return ins
    return link


def bc(ap, axis, n):
    ap = ap.unsqueeze(axis)
    shape = list(ap.shape)
    shape[axis] = n
    return ap.broadcast_to(shape)


def rows(dram, g):
    return dram.rearrange("(n p) d -> p n d", p=P)[:, bass.ds(g * TILES, TILES), :]


class Memory:

    def __init__(self, nc, ctx, prefix):
        self.nc, self.ctx, self.prefix = nc, ctx, prefix
        self.sems = []

    def sb(self, name, shape, dt=F32):
        return self.ctx.enter_context(self.nc.sbuf_tensor(f"{self.prefix}_{name}", shape, dt))

    def ps(self, name, shape):
        return self.ctx.enter_context(self.nc.psum_tensor(f"{self.prefix}_{name}", shape, F32))

    def sem(self, name):
        self.sems.append(self.nc.alloc_semaphore(name=f"{self.prefix}_{name}"))
        return self.sems[-1]

    def clear(self):
        self.nc.clear_and_free_semaphores(self.sems)
        self.nc.all_engine_barrier()


class LayerNorm:

    LINKS = 3

    def __init__(self, m):
        self.stats = m.sb("stats", [P, TILES, 6])
        self.sum = m.sb("ln_sum", [P, TILES])
        self.mean = m.sb("ln_mean", [P, TILES])
        self.diff = m.sb("ln_diff", [P, TILES])
        self.m2 = m.sb("ln_m2", [P, TILES])
        self.dm2 = m.sb("ln_dm2", [P, TILES])
        self.var_eps = m.sb("ln_var_eps", [P, TILES])
        self.rstd = m.sb("ln_rstd", [P, TILES])
        self.minus_half = m.sb("ln_minus_half", [P, TILES])


def layer_norm_stats(v, link, x, ln):
    for t in range(TILES):
        ins = v.bn_stats(ln.stats[:, t, :], x[:, t, :])
    link(ins)
    v.tensor_tensor(ln.sum[:, :], ln.stats[:, :, 1], ln.stats[:, :, 4], ALU.add)
    v.tensor_tensor(ln.diff[:, :], ln.stats[:, :, 1], ln.stats[:, :, 4], ALU.subtract)
    link(v.tensor_tensor(ln.m2[:, :], ln.stats[:, :, 2], ln.stats[:, :, 5], ALU.add))
    v.tensor_scalar(ln.mean[:, :], ln.sum[:, :], 0.5, None, ALU.mult)
    v.tensor_scalar(ln.m2[:, :], ln.m2[:, :], 1.0 / D, LN_EPS, ALU.mult, ALU.add)
    link(v.scalar_tensor_tensor(ln.dm2[:, :], ln.diff[:, :], 0.25, ln.diff[:, :], ALU.mult, ALU.mult))


def layer_norm_apply(v, x, ln, xn):
    for t in range(TILES):
        ins = v.tensor_scalar(xn[:, t, :], x[:, t, :], ln.mean[:, t:t + 1], ln.rstd[:, t:t + 1],
                              ALU.subtract, ALU.mult)
    return ins


def reach(eng, sem, value):
    if not (isinstance(value, int) and value <= 0):
        eng.wait_ge(sem, value)


def everything(t):
    return t[tuple(slice(None) for _ in t.shape)]


def sequence_rows(dram, half, g, n):
    return dram.rearrange("(s t u) d -> u s t d", u=2, t=BATCH // 2)[half, :, bass.ds(g * TILES, n * TILES), :]


def attention_phase(nc, pre, w, src, dst, ctxT, self_attn=False, guarded=False, prefetch=None):
    CLAMP = 10000.0
    C = D if self_attn else DC
    UNITS = 8
    SLOTS = 2 * UNITS
    STEPS = GROUPS // 2
    KEYS = SEQ
    LAG = 2
    SCALE = float(HD) ** -0.5
    HALF = P // 2
    with ExitStack() as ctx:
        m = Memory(nc, ctx, pre)
        ctx.callback(m.clear)
        wq = m.sb("wq", [D, P])
        wk = m.sb("wk", [C, P])
        wv = m.sb("wv", [C, 2, HALF])
        wo = m.sb("wo", [P, D])
        bq = m.sb("bq", [P, 1])
        bk = m.sb("bk", [P, 1])
        bv = m.sb("bv", [P, HALF])
        bo = m.sb("bo", [P, D])
        bq_scaled = m.sb("bq_scaled", [P, 4])
        q_scale = m.sb("q_scale", [P, 4])
        bk_masked = m.sb("bk_masked", [P, 4])
        mask = m.sb("mask", [P, 4])
        quarter = m.sb("quarter", [P, 4])
        ident = m.sb("ident", [P, P])
        x = m.sb("x", [P, GROUPS * TILES, D])
        kv = None if self_attn else m.sb("kv", [C, TOKENS])
        kvg = None if self_attn else m.sb("kvg", [C, GROUP])
        ln = LayerNorm(m)
        xn = m.sb("xn", [P, TILES, D])
        xnT = m.sb("xnT", [D, GROUP])
        qT = m.sb("qT", [P, 2, 4, GROUP])
        kT = m.sb("kT", [P, 2, 4, GROUP])
        v1 = m.sb("v1", [P, 2, TILES, HEADS // 2, 2, 2 * HD])
        ot_sb = m.sb("ot_sb", [P, 2, GROUP // 2])
        smax = m.sb("smax", [P, 4, 8])
        s_clip = m.sb("s_clip", [P, 2, GROUP]) if guarded else None
        s_sb = m.sb("s_sb", [P, 4, GROUP])
        pt_sb = m.sb("pt_sb", [P, 2, GROUP])
        rden = m.sb("rden", [P, 2, HEADS])
        on = m.sb("on", [P, 2, TILES, D])
        oT = m.sb("oT", [P, TOKENS if guarded else GROUP])

        pS = m.ps("pS", [P, 2, GROUP])
        pPT = m.ps("pPT", [P, GROUP])
        pOT = m.ps("pOT", [P, GROUP // 2])
        pO = m.ps("pO", [P, 2, GROUP])
        pM = m.ps("pM", [P, 2, GROUP])

        w_in, x_first, x_rest, kv_in = m.sem("w_in"), m.sem("x_first"), m.sem("x_rest"), m.sem("kv_in")
        consts, setup = m.sem("consts"), m.sem("setup")
        var_ready, rstd_ready, xn_ready = m.sem("var_ready"), m.sem("rstd_ready"), m.sem("xn_ready")
        xT_psum, xnT_ready, kvg_ready = m.sem("xT_psum"), m.sem("xnT_ready"), m.sem("kvg_ready")
        k_psum, k_ready, q_psum, q_ready = m.sem("k_psum"), m.sem("k_ready"), m.sem("q_psum"), m.sem("q_ready")
        v_psum, v_ready, xb_ready = m.sem("v_psum"), m.sem("v_ready"), m.sem("xb_ready")
        s_psum, clip_done, max_done, s_used = m.sem("s_psum"), m.sem("clip_done"), m.sem("max_done"), m.sem("s_used")
        exp_done, pt_psum, pt_ready = m.sem("exp_done"), m.sem("pt_psum"), m.sem("pt_ready")
        pv_psum, po_ready, o_psum = m.sem("pv_psum"), m.sem("po_ready"), m.sem("o_psum")
        o_used, rden_done = m.sem("o_used"), m.sem("rden_done")
        ot_psum, ot_ready, y_psum, y_done = m.sem("ot_psum"), m.sem("ot_ready"), m.sem("y_psum"), m.sem("y_done")
        x_out, chain, guard, nan_added = m.sem("x_out"), m.sem("chain"), m.sem("guard"), m.sem("nan_added")
        flag_psum = m.sem("flag_psum")

        block = ctx.enter_context(nc.Block())
        NW = 12

        if guarded:
            nan_sum = m.sb("nan_sum", [P, GROUP])
            nan_col = m.sb("nan_col", [P, 4])
            nan_mask = m.sb("nan_mask", [P, 1])
            ones = m.sb("ones", [P, P])
            kv_mean = m.sb("kv_mean", [C, BATCH])
            wv_all = m.sb("wv_all", [C, P])
            bv_col = m.sb("bv_col", [P, 1])
            v_mean = m.sb("v_mean", [P, BATCH])
            NW += 2

        def two_groups(eng, step):
            step(0, True, False)
            with eng.Fori(1, STEPS - 1) as i:
                step(i, False, False)
            step(STEPS - 1, False, True)

        def at_most(count):
            return min(count, GROUPS) if isinstance(count, int) else count

        def xg(g):
            return x[:, bass.ds(g * TILES, TILES), :]

        loads = [(ident, "ident"), (wq, pre + "_wq"), (wk, pre + "_wk"), (wv, pre + "_wv"), (wo, pre + "_wo"),
                 (bq, pre + "_bq"), (bk, pre + "_bk"), (mask, "mask"), (quarter, "quarter")]
        if guarded:
            loads += [(wv_all, pre + "_wv_all"), (bv_col, pre + "_bv_col")]

        @block.sync
        def _(sp):
            def load(g, n, sem):
                if self_attn:
                    for half in range(2):
                        sp.dma_start(x[half * HALF:(half + 1) * HALF, g * TILES:(g + n) * TILES, :],
                                     sequence_rows(src, half, g, n)).then_inc(sem, 16)
                else:
                    sp.dma_start(x[:, g * TILES:(g + n) * TILES, :],
                                 src.rearrange("(n p) d -> p n d", p=P)[:, g * TILES:(g + n) * TILES, :]
                                 ).then_inc(sem, 16)

            load(0, 1, x_first)
            if not self_attn:
                sp.dma_start(kv[:, :], ctxT).then_inc(kv_in, 16)
            for buf, name in loads[0::2]:
                sp.dma_start(everything(buf), w[name]).then_inc(w_in, 16)
            load(1, GROUPS - 1, x_rest)
            if prefetch:
                prefetch.load(sp)

            def store(g):
                sp.wait_ge(y_done, g + 1)
                if self_attn:
                    for half in range(2):
                        sp.dma_start(sequence_rows(dst, half, g, 1),
                                     x[half * HALF:(half + 1) * HALF, bass.ds(g * TILES, TILES), :]
                                     ).then_inc(x_out, 16)
                else:
                    sp.dma_start(rows(dst, g), xg(g)).then_inc(x_out, 16)

            sp.wait_ge(x_first, 16 * (2 if self_attn else 1))
            sp.wait_ge(x_rest, 16 * (2 if self_attn else 1))
            with sp.Fori(0, GROUPS) as g:
                store(g)
            sp.wait_ge(x_out, 16 * GROUPS * (2 if self_attn else 1))
            if prefetch:
                prefetch.wait(sp)

        @block.gpsimd
        def _(pool):
            pool.memset(ln.minus_half[:, :], -0.5).then_inc(consts, 1)
            pool.memset(everything(v1), 1.0).then_inc(consts, 1)
            if guarded:
                pool.memset(ones[:, :], 1.0).then_inc(consts, 1)
                pool.memset(nan_sum[:, :], 0.0).then_inc(consts, 1)
            pool.wait_ge(consts, 4 if guarded else 2)

            def rstd(g):
                pool.wait_ge(var_ready, g + 1)
                pool.tensor_tensor(ln.rstd[:, :], ln.var_eps[:, :], ln.minus_half[:, :],
                                   ALU.pow).then_inc(rstd_ready, 1)

            def add_bias(g):
                pool.wait_ge(xn_ready, g + 1)
                pool.tensor_tensor(xg(g), xg(g), bc(bo[:, :], 1, TILES), ALU.add).then_inc(xb_ready, 1)

            def nan_sums(g, par):
                pool.wait_ge(q_ready, g + 1)
                pool.tensor_tensor(nan_sum[:, :], nan_sum[:, :], qT[:, par, 0, :], ALU.add).then_inc(nan_added, 1)
                pool.wait_ge(nan_added, 2 * g + 1)
                pool.wait_ge(k_ready, g + 1)
                pool.tensor_tensor(nan_sum[:, :], nan_sum[:, :], kT[:, par, 0, :], ALU.add).then_inc(nan_added, 1)
                pool.wait_ge(nan_added, 2 * g + 2)

            rstd(0)
            pool.wait_ge(w_in, 16 * NW)
            rstd(1)
            add_bias(0)
            if guarded:
                nan_sums(0, 0)

            def step(i, first, last):
                for s in range(SLOTS):
                    c, u = 2 * i + s // UNITS, s % UNITS
                    if guarded and u == 5 and not (last and s >= UNITS):
                        nan_sums(c + 1, 1 - s // UNITS)
                    if u == 5 and not last:
                        rstd(c + 2)
                    if u == 6 and not (last and s >= UNITS):
                        add_bias(c + 1)
            two_groups(pool, step)

        @block.vector
        def _(v):
            def layer_norm(g, link):
                if isinstance(g, int) and g == 0:
                    v.wait_ge(x_first, 16 * (2 if self_attn else 1))
                elif isinstance(g, int) and g == 1:
                    v.wait_ge(x_rest, 16 * (2 if self_attn else 1))
                layer_norm_stats(v, link, xg(g), ln)
                v.tensor_tensor(ln.var_eps[:, :], ln.m2[:, :], ln.dm2[:, :], ALU.add).then_inc(var_ready, 1)

            def normal(g):
                reach(v, xT_psum, g)
                v.wait_ge(rstd_ready, g + 1)
                layer_norm_apply(v, xg(g), ln, xn).then_inc(xn_ready, 1)
                v.wait_ge(xn_ready, g + 1)

            base = 1 if guarded else 0
            link = linker(v, Count(chain, 0))
            v.wait_ge(consts, 4 if guarded else 2)
            layer_norm(0, link)
            normal(0)
            v.wait_ge(w_in, 16 * NW)
            v.tensor_scalar(bq_scaled[:, :], quarter[:, :], bq[:, 0:1], SCALE, ALU.mult, ALU.mult)
            v.tensor_scalar(q_scale[:, :], quarter[:, :], SCALE, None, ALU.mult)
            v.tensor_scalar(bk_masked[:, :], mask[:, :], bk[:, 0:1], None, ALU.mult).then_inc(setup, 1)

            def value_bias(g, par):
                v.wait_ge(v_psum, g + 1)
                reach(v, pv_psum, (g - 1) * UNITS)
                for b in range(2):
                    ins = v.tensor_tensor(v1[:, par, :, :, b, 0:HD],
                                          pM[:, 1, :].rearrange("p (t b i d) -> p t b i d", b=2, i=HEADS // 2,
                                                                d=HD)[:, :, b],
                                          bc(bv[:, :], 1, TILES).rearrange("p t (i d) -> p t i d", d=HD), ALU.add)
                ins.then_inc(v_ready, 1)

            def less_max(n, s):
                sc = s_clip[:, s % 2, :] if guarded else pS[:, s % 2, :]
                v.wait_ge(max_done, n + 1)
                reach(v, pt_psum, n - 3)
                v.tensor_tensor(s_sb[:, s % 4, :].rearrange("p (h k) -> p h k", k=KEYS),
                                sc.rearrange("p (h k) -> p h k", k=KEYS), bc(smax[:, s % 4, :], 2, KEYS),
                                ALU.subtract).then_inc(s_used, 1)

            def scores(n, s, first_unit):
                v.wait_ge(s_psum, n + 1)
                sc = pS[:, s % 2, :]
                if guarded:
                    reach(v, s_used, n - 1)
                    v.tensor_scalar(s_clip[:, s % 2, :], sc, -CLAMP, CLAMP, ALU.max, ALU.min).then_inc(clip_done, 1)
                    if not first_unit:
                        less_max(n - 1, s - 1)
                    v.wait_ge(clip_done, n + 1)
                    sc = s_clip[:, s % 2, :]
                v.tensor_reduce(smax[:, s % 4, :], sc.rearrange("p (h k) -> p h k", k=KEYS), AX.X,
                                ALU.max).then_inc(max_done, 1)
                if not guarded:
                    less_max(n, s)

            def normalise(pp, g, k, par):
                v.wait_ge(o_psum, (pp + 1) * 4)
                if k == 0:
                    reach(v, ot_psum, g - 1)
                for b in range(2):
                    lo, hi = b * HALF, (b + 1) * HALF
                    o = pO[lo:hi, :, :].rearrange("p t (h b d) -> p t h b d", h=HEADS, b=2)[:, :, :, b]
                    ins = v.reciprocal(rden[lo:hi, :, :], o[:, :, :, HD])
                ins.then_inc(rden_done, 1)
                v.wait_ge(rden_done, pp + 1)
                for b in range(2):
                    lo, hi = b * HALF, (b + 1) * HALF
                    o = pO[lo:hi, :, :].rearrange("p t (h b d) -> p t h b d", h=HEADS, b=2)[:, :, :, b]
                    ins = v.tensor_tensor(on[lo:hi, par, 2 * k:2 * k + 2, :].rearrange("p t (h d) -> p t h d", d=HD),
                                          o[:, :, :, 0:HD], bc(rden[lo:hi, :, :], 3, HD), ALU.mult)
                ins.then_inc(o_used, 1)

            def residual(g):
                v.wait_ge(xb_ready, g + 1)
                v.wait_ge(y_psum, g + 1)
                v.tensor_tensor(xg(g), pM[:, 1, :].rearrange("p (t d) -> p t d", d=D), xg(g),
                                ALU.add).then_inc(y_done, 1)

            layer_norm(1, link)
            normal(1)
            value_bias(0, 0)
            if guarded:
                v.wait_ge(kv_in, 16)
                link(v.tensor_reduce(kv_mean[:, :], kv[:, :].rearrange("c (b k) -> c b k", k=KEYS), AX.X, ALU.add))
                v.tensor_scalar(kv_mean[:, :], kv_mean[:, :], 1.0 / KEYS, None, ALU.mult).then_inc(guard, 1)
            LINKS = ln.LINKS

            def step(i, first, last):
                for s in range(SLOTS):
                    half, u = s // UNITS, s % UNITS
                    c = 2 * i + half
                    n = i * SLOTS + s
                    scores(n, s, first and s == 0)
                    if s % 4 == (LAG + 1) % 4 and not (first and s < LAG + 5):
                        pair = (s - LAG - 1) // 4 - 1
                        normalise(4 * i + pair, 2 * i + pair // 2, pair % 2, (pair // 2) % 2)
                    if u == 4 and not (last and half == 1):
                        value_bias(c + 1, 1 - half)
                    if u == 5 and not last:
                        link = linker(v, Count(chain, base + (c + 2) * LINKS))
                        layer_norm(c + 2, link)
                    if u == 6 and not last:
                        normal(c + 2)
                    if u == 7 and not (first and half == 0) and not guarded:
                        residual(c - 1)

            two_groups(v, step)
            if guarded:
                less_max(GROUPS * UNITS - 1, SLOTS - 1)
            normalise(2 * GROUPS - 1, GROUPS - 1, 1, 1)
            if not guarded:
                residual(GROUPS - 1)
            else:
                v.wait_ge(nan_added, 2 * GROUPS)
                v.tensor_scalar(nan_sum[:, :], nan_sum[:, :], 0.0, None, ALU.mult).then_inc(guard, 1)
                v.wait_ge(guard, 2)
                v.tensor_reduce(nan_col[:, 0:1], nan_sum[:, :], AX.X, ALU.add).then_inc(guard, 1)
                v.wait_ge(flag_psum, 1)
                v.tensor_copy(nan_col[:, 1:2], pO[:, 0, 0:1]).then_inc(guard, 1)
                v.wait_ge(guard, 4)
                v.tensor_tensor(nan_mask[:, :], nan_col[:, 1:2], nan_col[:, 1:2], ALU.not_equal)
                v.tensor_scalar(v_mean[:, :], pO[:, 1, 0:BATCH], bv_col[:, 0:1], None, ALU.add).then_inc(guard, 1)
                v.wait_ge(guard, 5)
                v.wait_ge(ot_ready, GROUPS)
                v.copy_predicated(oT[:, :], bc(nan_mask[:, 0:1].bitcast(I32)[:, 0], 1, TOKENS),
                                  bc(v_mean[:, :], 2, KEYS)).then_inc(guard, 1)
                for g in range(GROUPS):
                    v.wait_ge(y_psum, g + 1)
                    v.wait_ge(xb_ready, g + 1)
                    v.tensor_tensor(xg(g), pM[:, g % 2, :].rearrange("p (t d) -> p t d", d=D), xg(g),
                                    ALU.add).then_inc(y_done, 1)

        @block.scalar
        def _(act):
            for buf, name in loads[1::2]:
                act.dma_start(everything(buf), w[name]).then_inc(w_in, 16)
            for half in range(2):
                act.dma_start(bv[half * HALF:(half + 1) * HALF, :],
                              w[pre + "_bv"][half].partition_broadcast(HALF)).then_inc(w_in, 16)
            act.dma_start(bo[:, :], w[pre + "_bo"].partition_broadcast(P)).then_inc(w_in, 16)
            act.wait_ge(w_in, 16 * NW)
            act.wait_ge(setup, 1)

            def copy_xT(g):
                if self_attn:
                    reach(act, v_psum, g)
                reach(act, q_psum, g)
                act.wait_ge(xT_psum, g + 1)
                act.activation(xnT[:, :], pM[:, 0, :], ACT.Identity).then_inc(xnT_ready, 1)

            def copy_kv(g):
                if not self_attn:
                    act.wait_ge(kv_in, 16)
                    reach(act, v_psum, g)
                    act.activation(kvg[:, :], kv[:, bass.ds(g * GROUP, GROUP)], ACT.Identity).then_inc(kvg_ready, 1)

            def copy_k(g, par):
                act.wait_ge(k_psum, g + 1)
                reach(act, s_psum, (g - 1) * UNITS)
                if guarded:
                    reach(act, nan_added, 2 * g - 2)
                for j in range(4):
                    ins = act.activation(kT[:, par, j, :], pM[:, 1, :], ACT.Identity, bias=bk_masked[:, j:j + 1],
                                         scale=mask[:, j:j + 1])
                ins.then_inc(k_ready, 1)

            def copy_q(g, par):
                act.wait_ge(q_psum, g + 1)
                reach(act, s_psum, (g - 1) * UNITS)
                if guarded:
                    reach(act, nan_added, 2 * g - 2)
                for r in range(4):
                    ins = act.activation(qT[:, par, r, :], pM[:, 0, :], ACT.Identity, bias=bq_scaled[:, r:r + 1],
                                         scale=q_scale[:, r:r + 1])
                ins.then_inc(q_ready, 1)

            def exponent(n, s):
                act.wait_ge(s_used, n + 1)
                act.activation(s_sb[:, s % 4, :], s_sb[:, s % 4, :], ACT.Exp).then_inc(exp_done, 1)

            def copy_pt(n, s):
                act.wait_ge(pt_psum, n + 1)
                reach(act, pv_psum, n - 1)
                act.activation(pt_sb[:, s % 2, :], pPT[:, :], ACT.Identity).then_inc(pt_ready, 1)

            def copy_po(n, s):
                act.wait_ge(pv_psum, n + 1)
                reach(act, o_psum, n - 1)
                act.activation(ot_sb[:, s % 2, :], pOT[:, :], ACT.Identity).then_inc(po_ready, 1)

            def copy_oT(g):
                act.wait_ge(ot_psum, g + 1)
                if guarded:
                    out = oT[:, bass.ds(g * GROUP, GROUP)]
                else:
                    reach(act, y_psum, g)
                    out = oT[:, :]
                act.activation(out, pM[:, 0, :], ACT.Identity).then_inc(ot_ready, 1)

            copy_kv(0)
            copy_xT(0)
            copy_k(0, 0)
            copy_q(0, 0)
            if not self_attn:
                copy_kv(1)

            def step(i, first, last):
                for s in range(SLOTS):
                    half, u = s // UNITS, s % UNITS
                    c = 2 * i + half
                    n = i * SLOTS + s
                    if not (first and s < 1):
                        exponent(n - 1, s - 1)
                    if not (first and s < LAG):
                        copy_pt(n - LAG, s - LAG)
                    if not (first and s < LAG + 1):
                        copy_po(n - LAG - 1, s - LAG - 1)
                    if not (last and half == 1):
                        if u == 0:
                            copy_xT(c + 1)
                        if u == 2:
                            copy_k(c + 1, 1 - half)
                        if u == 3:
                            copy_q(c + 1, 1 - half)
                        if u == 6 and not (last and half == 0) and not self_attn:
                            copy_kv(c + 2)
                    if u == 5 and not (first and half == 0):
                        copy_oT(c - 1)
            two_groups(act, step)
            N = GROUPS * UNITS
            exponent(N - 1, N - 1)
            for k in range(N - LAG, N + 1):
                if k < N:
                    copy_pt(k, k)
                copy_po(k - 1, k - 1)
            copy_oT(GROUPS - 1)

        @block.tensor
        def _(pe):
            pe.wait_ge(w_in, 16 * NW)
            pe.wait_ge(consts, 4 if guarded else 2)

            def turn_x(g):
                pe.wait_ge(xn_ready, g + 1)
                reach(pe, ot_ready, g - 2)
                for t in range(TILES):
                    ins = pe.transpose(pM[:, 0, t * P:(t + 1) * P], xn[:, t, :], ident[:, :])
                ins.then_inc(xT_psum, 1)

            def project_k(g):
                if self_attn:
                    pe.wait_ge(xnT_ready, g + 1)
                else:
                    pe.wait_ge(kvg_ready, g + 1)
                if guarded:
                    reach(pe, v_ready, g)
                else:
                    reach(pe, y_done, g - 2)
                    reach(pe, v_ready, g)
                pe.matmul(pM[:, 1, :], wk[:, :], (xnT if self_attn else kvg)[:, :],
                          start=True, stop=True).then_inc(k_psum, 1)

            def project_q(g):
                pe.wait_ge(xnT_ready, g + 1)
                pe.matmul(pM[:, 0, :], wq[:, :], xnT[:, :], start=True, stop=True).then_inc(q_psum, 1)

            def project_v(g):
                pe.wait_ge(k_ready, g + 1)
                kvT = xnT if self_attn else kvg
                for b in range(2 * TILES):
                    for hl in range(2):
                        ins = pe.matmul(pM[hl * HALF:(hl + 1) * HALF, 1, b * HALF:(b + 1) * HALF],
                                        kvT[:, b * SEQ:(b + 1) * SEQ], wv[:, hl, :], start=True, stop=True)
                ins.then_inc(v_psum, 1)

            def scores(n, s, par):
                pp, r = (s // 4) % 2, s % 4
                reach(pe, clip_done if guarded else s_used, n - 1)
                for pl in range(2):
                    for b in range(2):
                        t0 = (2 * pp + pl) * P + b * SEQ
                        ins = pe.matmul(pS[b * HALF:(b + 1) * HALF, s % 2, pl * 256:(pl + 1) * 256],
                                        qT[:, par, r, t0:t0 + SEQ], kT[:, par, :, t0:t0 + SEQ],
                                        start=True, stop=True)
                ins.then_inc(s_psum, 1)

            def turn_weights(n, s):
                pe.wait_ge(exp_done, n + 1)
                reach(pe, pt_ready, n)
                for k in range(4):
                    ins = pe.transpose(pPT[:, k * P:(k + 1) * P], s_sb[:, s % 4, k * P:(k + 1) * P],
                                       ident[:, :])
                ins.then_inc(pt_psum, 1)

            def weights_times_v(n, s, par):
                pp, r = (s // 4) % 2, s % 4
                for pl in range(2):
                    for jj in range(2):
                        for hl in range(2):
                            q, lo, hi = 2 * jj + hl, hl * HALF, (hl + 1) * HALF
                            ins = pe.matmul(pOT[32 * q:32 * q + 32, pl * P:(pl + 1) * P],
                                            v1[lo:hi, par, 2 * pp + pl, 2 * r + jj, :, :].rearrange("p b d -> p (b d)"),
                                            pt_sb[lo:hi, s % 2, (pl * 2 + jj) * P:(pl * 2 + jj + 1) * P],
                                            start=True, stop=True)
                ins.then_inc(pv_psum, 1)

            def turn_outputs(n, s, pp):
                r = s % 4
                pe.wait_ge(po_ready, n + 1)
                if r == 0:
                    reach(pe, o_used, pp)
                for pl in range(2):
                    ins = pe.transpose(pO[:, pl, r * P:(r + 1) * P], ot_sb[:, s % 2, pl * P:(pl + 1) * P],
                                       ident[:, :])
                ins.then_inc(o_psum, 1)

            def turn_o(g, par):
                pe.wait_ge(o_used, 2 * g + 2)
                pe.wait_ge(q_ready, at_most(g + 3))
                if isinstance(g, int) and g == GROUPS - 1:
                    pe.wait_ge(ot_ready, g)
                for t in range(TILES):
                    ins = pe.transpose(pM[:, 0, t * P:(t + 1) * P], on[:, par, t, :], ident[:, :])
                ins.then_inc(ot_psum, 1)

            def project_o(g):
                pe.wait_ge(ot_ready, g + 1)
                pe.wait_ge(v_ready, at_most(g + 3))
                if isinstance(g, int) and g == GROUPS - 1:
                    pe.wait_ge(y_done, g)
                for t in range(TILES):
                    ins = pe.matmul(pM[:, 1, t * P:(t + 1) * P], oT[:, t * P:(t + 1) * P], wo[:, :],
                                    start=True, stop=True)
                ins.then_inc(y_psum, 1)

            turn_x(0)
            project_k(0)
            project_q(0)
            project_v(0)
            pe.wait_ge(q_ready, 1)
            pe.wait_ge(v_ready, 1)

            def step(i, first, last):
                for s in range(SLOTS):
                    half, u = s // UNITS, s % UNITS
                    c = 2 * i + half
                    n = i * SLOTS + s
                    if u == 0:
                        pe.wait_ge(q_ready, c + 1)
                    scores(n, s, half)
                    if u == LAG + 1:
                        pe.wait_ge(v_ready, c + 1)
                    if not (first and s < LAG + 2):
                        pe.wait_ge(po_ready, n - LAG - 1)
                    if not (first and s < LAG):
                        turn_weights(n - LAG, (s - LAG) % SLOTS)
                    if not (first and s < LAG + 1):
                        q = (s - LAG - 1) % SLOTS
                        weights_times_v(n - LAG - 1, q, q // UNITS)
                    if not (first and s < LAG + 2):
                        turn_outputs(n - LAG - 2, (s - LAG - 2) % SLOTS, 4 * i + (s - LAG - 2) // 4)
                    if not (last and half == 1):
                        if u == 0:
                            turn_x(c + 1)
                        if u == 2:
                            project_k(c + 1)
                        if u == 3:
                            project_q(c + 1)
                        if u == 4:
                            project_v(c + 1)
                    if u == 5 and not (first and half == 0):
                        turn_o(c - 1, 1 - half)
                    if u == 6 and not (first and half == 0) and not guarded:
                        project_o(c - 1)
            two_groups(pe, step)
            N = GROUPS * UNITS
            for k in range(N - LAG, N + 1):
                pe.wait_ge(po_ready, k - 1)
                if k < N:
                    turn_weights(k, k % 16)
                else:
                    pe.wait_ge(pt_ready, N)
                weights_times_v(k - 1, (k - 1) % 16, 1)
                turn_outputs(k - 2, (k - 2) % 16, (k - 2) // 4)
            turn_outputs(N - 1, 15, 15)
            turn_o(GROUPS - 1, 1)
            if not guarded:
                project_o(GROUPS - 1)
            else:
                pe.wait_ge(guard, 3)
                pe.wait_ge(o_used, 16)
                pe.matmul(pO[:, 0, 0:1], ones[:, :], nan_col[:, 0:1], start=True, stop=True)
                pe.matmul(pO[:, 1, 0:BATCH], wv_all[:, :], kv_mean[:, :], start=True, stop=True).then_inc(flag_psum, 1)
                pe.wait_ge(guard, 6)
                for g in range(GROUPS):
                    reach(pe, y_done, g - 1)
                    for t in range(TILES):
                        t0 = g * GROUP + t * P
                        ins = pe.matmul(pM[:, g % 2, t * P:(t + 1) * P], oT[:, t0:t0 + P], wo[:, :],
                                        start=True, stop=True)
                    ins.then_inc(y_psum, 1)


def mamba_phase(nc, pre, w, src, dst):
    N = 16
    RANK = 8
    TAPS = 4
    EXP_AND_LN = "natural_log_exp_and_others"
    PAD = TAPS - 1
    SEQS = GROUP // SEQ
    SLOTS = 2 * N
    STEPS = GROUPS // 2
    XD = 2 * N + RANK
    AHEAD = 3
    with ExitStack() as ctx:
        m = Memory(nc, ctx, pre)
        ctx.callback(m.clear)
        ident = m.sb("ident", [P, P])
        w_in_t = m.sb("w_in_t", [D, 4, P])
        conv_w = m.sb("conv_w", [P, TAPS, 2, P])
        w_taps = m.sb("w_taps", [D, TAPS, 2, P])
        conv_b = m.sb("conv_b", [P, 2])
        w_x = m.sb("w_x", [P, 2, XD])
        w_dt = m.sb("w_dt", [RANK, 2, P])
        b_dt = m.sb("b_dt", [P, 2])
        a_neg = m.sb("a_neg", [P, 2, N])
        d_skip = m.sb("d_skip", [P, 2])
        w_out_t = m.sb("w_out_t", [P, 2, D])
        sel = m.sb("sel", [3 * 2 * N, 2 * N])
        sel_bf = m.sb("sel_bf", [3 * 2 * N, 2 * N, P], BF16)
        x = m.sb("x", [P, GROUPS * TILES, D])
        ln = LayerNorm(m)
        xn = m.sb("xn", [P, TILES, D])
        xnT = m.sb("xnT", [D, SEQS, PAD + SEQ])
        z = m.sb("z", [P, 2, GROUP])
        z_gate = m.sb("z_gate", [P, 2, GROUP])
        xs = m.sb("xs", [P, 2, 2, GROUP])
        dt_low = m.sb("dt_low", [RANK, GROUP])
        rest = m.sb("rest", [P, GROUP])
        split = m.sb("split", [3 * 2 * N, 2, GROUP], BF16)
        absv = m.sb("absv", [P, 2, GROUP])
        e1 = m.sb("e1", [P, 2, GROUP])
        e1p = m.sb("e1p", [P, 2, GROUP])
        lnv = m.sb("lnv", [P, 2, GROUP])
        relu = m.sb("relu", [P, 2, GROUP])
        dt = m.sb("dt", [P, 2, 2, GROUP])
        u = m.sb("u", [P, 2, 2, GROUP])
        dA = m.sb("dA", [P, 4, 2, SEQS, SEQ])
        b_sb = m.sb("b_sb", [P, 4, GROUP])
        dbx = m.sb("dbx", [P, 4, 2, GROUP])
        h = m.sb("h", [P, 2, 2, GROUP])
        hc = m.sb("hc", [P, 4, 2, GROUP])
        y_skip = m.sb("y_skip", [P, 2, GROUP])
        y_gated = m.sb("y_gated", [P, 2, GROUP])

        pB = m.ps("pB", [P, 2, GROUP])
        pC = m.ps("pC", [P, 2, GROUP])
        pY = m.ps("pY", [P, 2, GROUP])
        pM = m.ps("pM", [P, 2, GROUP])

        (w_in, x_first, x_rest, consts, chain, setup, a_exp) = [
            m.sem(k) for k in ("w_in", "x_first", "x_rest", "consts", "chain", "setup", "a_exp")]
        var_ready, rstd_ready, xn_ready = m.sem("var_ready"), m.sem("rstd_ready"), m.sem("xn_ready")
        xT_psum, xnT_ready, z_psum, z_ready = m.sem("xT_psum"), m.sem("xnT_ready"), m.sem("z_psum"), m.sem("z_ready")
        xs_psum, zg_ready, xs_ready = m.sem("xs_psum"), m.sem("zg_ready"), m.sem("xs_ready")
        xd_psum, hi_ready, low_ready = m.sem("xd_psum"), m.sem("hi_ready"), m.sem("low_ready")
        rest_ready, mid_ready, split_ready = m.sem("rest_ready"), m.sem("mid_ready"), m.sem("split_ready")
        dt_psum, soft_link, ln_ready, relu_ready = m.sem("dt_psum"), m.sem("soft_link"), m.sem("ln_ready"), m.sem("relu_ready")
        err_ready, fix_ready, dt_ready, u_ready = m.sem("err_ready"), m.sem("fix_ready"), m.sem("dt_ready"), m.sem("u_ready")
        da_ready, b_psum, b_ready, dbx_ready = m.sem("da_ready"), m.sem("b_psum"), m.sem("b_ready"), m.sem("dbx_ready")
        scan_done, c_psum, hc_ready, y_psum = m.sem("scan_done"), m.sem("c_psum"), m.sem("hc_ready"), m.sem("y_psum")
        y_used, y_ready, o_psum, o_done, x_out = m.sem("y_used"), m.sem("y_ready"), m.sem("o_psum"), m.sem("o_done"), m.sem("x_out")

        block = ctx.enter_context(nc.Block())
        NW = 11

        def two_groups(eng, step):
            step(0, True, False)
            with eng.Fori(1, STEPS - 1) as i:
                step(i, False, False)
            step(STEPS - 1, False, True)

        def at_most(count):
            return min(count, GROUPS) if isinstance(count, int) else count

        def xg(g):
            return x[:, bass.ds(g * TILES, TILES), :]

        @block.sync
        def _(sp):
            def load(g, n, sem):
                sp.dma_start(x[:, g * TILES:(g + n) * TILES, :],
                             src.rearrange("(n p) d -> p n d", p=P)[:, g * TILES:(g + n) * TILES, :]
                             ).then_inc(sem, 16)

            load(0, 1, x_first)
            for buf, name in ((ident, "ident"), (w_in_t, "w_in_t"), (conv_b, "conv_b"), (w_x, "w_x"),
                              (w_dt, "w_dt"), (b_dt, "b_dt"), (a_neg, "a_log"), (d_skip, "d_skip"),
                              (w_out_t, "w_out_t"), (sel, "sel")):
                sp.dma_start(everything(buf), w[name if name == "ident" else f"{pre}_{name}"]).then_inc(w_in, 16)
            sp.dma_start(conv_w[:, :, :, :], w[pre + "_conv_w"].partition_broadcast(P)).then_inc(w_in, 16)
            load(1, GROUPS - 1, x_rest)
            sp.wait_ge(x_first, 16)
            sp.wait_ge(x_rest, 16)
            with sp.Fori(0, GROUPS) as g:
                sp.wait_ge(o_done, g + 1)
                sp.dma_start(rows(dst, g), xg(g)).then_inc(x_out, 16)
            sp.wait_ge(x_out, 16 * GROUPS)

        @block.gpsimd
        def _(pool):
            pool.memset(ln.minus_half[:, :], -0.5).then_inc(consts, 1)
            pool.memset(dA[:, :, :, :, 0:1], 0.0).then_inc(consts, 1)
            pool.memset(xnT[:, :, 0:PAD], 0.0).then_inc(consts, 1)
            pool.wait_ge(consts, 3)

            def rstd(g):
                pool.wait_ge(var_ready, g + 1)
                pool.tensor_tensor(ln.rstd[:, :], ln.var_eps[:, :], ln.minus_half[:, :],
                                   ALU.pow).then_inc(rstd_ready, 1)

            def soft_fix(g):
                pool.wait_ge(ln_ready, g + 1)
                pool.wait_ge(err_ready, g + 1)
                pool.tensor_tensor(lnv[:, :, :], lnv[:, :, :], e1[:, :, :], ALU.subtract).then_inc(fix_ready, 1)

            def times_b(k, s):
                pool.wait_ge(b_ready, k + 1)
                reach(pool, scan_done, k - 3)
                pool.tensor_tensor(dbx[:, s % 4, :, :], u[:, s // N, :, :], bc(b_sb[:, s % 4, :], 1, 2),
                                   ALU.mult).then_inc(dbx_ready, 1)

            rstd(0)
            rstd(1)
            soft_fix(0)

            def step(i, first, last):
                for s in range(SLOTS):
                    c, n = 2 * i + s // N, s % N
                    if n == 0:
                        pool.wait_ge(u_ready, c + 1)
                    times_b(i * SLOTS + s, s)
                    if n == 14 and not last:
                        rstd(c + 2)
                    if n == 14 and not (last and s >= N):
                        soft_fix(c + 1)
            two_groups(pool, step)

        @block.vector
        def _(v):
            v.wait_ge(consts, 3)
            v.wait_ge(x_first, 16)

            def layer_norm(g, link):
                if isinstance(g, int) and g == 1:
                    v.wait_ge(x_rest, 16)
                layer_norm_stats(v, link, xg(g), ln)
                v.tensor_tensor(ln.var_eps[:, :], ln.m2[:, :], ln.dm2[:, :], ALU.add).then_inc(var_ready, 1)

            def normalised(g):
                reach(v, xT_psum, g)
                v.wait_ge(rstd_ready, g + 1)
                layer_norm_apply(v, xg(g), ln, xn).then_inc(xn_ready, 1)
                v.wait_ge(xn_ready, g + 1)

            def split_rest(g, par):
                v.wait_ge(hi_ready, g + 1)
                v.tensor_tensor(rest[32:64, :], pM[0:32, 0, :], split[0:32, par, :],
                                ALU.subtract).then_inc(rest_ready, 1)

            def split_last(g, par):
                v.wait_ge(mid_ready, g + 1)
                v.tensor_tensor(split[64:96, par, :], rest[32:64, :], split[32:64, par, :],
                                ALU.subtract).then_inc(split_ready, 1)

            def rounding_of_1p(g):
                v.wait_ge(soft_link, 2 * g + 2)
                v.scalar_tensor_tensor(e1[:, :, :], e1p[:, :, :], -1.0, e1[:, :, :], ALU.add,
                                       ALU.subtract).then_inc(err_ready, 1)

            def make_dt(g, par):
                reach(v, da_ready, (g - 1) * N)
                v.wait_ge(fix_ready, g + 1)
                v.wait_ge(relu_ready, g + 1)
                v.tensor_tensor(dt[:, par, :, :], lnv[:, :, :], relu[:, :, :], ALU.add).then_inc(dt_ready, 1)

            def make_u(g, par):
                v.wait_ge(dt_ready, g + 1)
                v.wait_ge(xs_ready, g + 1)
                reach(v, dbx_ready, (g - 1) * N)
                v.tensor_tensor(u[:, par, :, :], dt[:, par, :, :], xs[:, par, :, :], ALU.mult).then_inc(u_ready, 1)

            def scan(k, s):
                v.wait_ge(da_ready, k + 1)
                v.wait_ge(dbx_ready, k + 1)
                reach(v, hc_ready, k - 1)
                v.tensor_tensor_scan(h[:, s % 2, :, :].rearrange("p a t -> p (a t)"),
                                     dA[:, s % 4, :, :, :].rearrange("p a b t -> p (a b t)"),
                                     dbx[:, s % 4, :, :].rearrange("p a t -> p (a t)"),
                                     0.0, ALU.mult, ALU.add).then_inc(scan_done, 1)

            def times_c(k, s):
                v.wait_ge(scan_done, k + 1)
                v.wait_ge(c_psum, k + 1)
                reach(v, y_psum, k - 3)
                v.tensor_tensor(hc[:, s % 4, :, :], h[:, s % 2, :, :], bc(pC[:, s % 2, :], 1, 2),
                                ALU.mult).then_inc(hc_ready, 1)

            def skip(g, par):
                v.wait_ge(y_psum, (g + 1) * N)
                reach(v, y_ready, g)
                for half in range(2):
                    ins = v.scalar_tensor_tensor(y_skip[:, half, :], xs[:, par, half, :], d_skip[:, half:half + 1],
                                                 pY[:, half, :], ALU.mult, ALU.add)
                ins.then_inc(y_used, 1)

            def gate(g, par):
                v.wait_ge(y_used, g + 1)
                v.wait_ge(zg_ready, g + 1)
                reach(v, o_psum, g)
                v.tensor_tensor(y_gated[:, :, :], y_skip[:, :, :], z_gate[:, :, :], ALU.mult).then_inc(y_ready, 1)

            def residual(g):
                v.wait_ge(o_psum, g + 1)
                v.tensor_tensor(xg(g), pM[:, 1, :].rearrange("p (t d) -> p t d", d=D), xg(g),
                                ALU.add).then_inc(o_done, 1)

            link = linker(v, Count(chain, 0))
            layer_norm(0, link)
            normalised(0)
            v.wait_ge(w_in, 16 * NW)
            v.tensor_tensor(w_taps[:, :, :, :], conv_w[:, :, :, :], bc(w_in_t[:, 0:2, :], 1, TAPS), ALU.mult)
            v.tensor_copy(sel_bf[:, :, :], bc(sel[:, :], 2, P))
            v.wait_ge(a_exp, 1)
            v.tensor_scalar(a_neg[:, :, :], a_neg[:, :, :], -1.0, None, ALU.mult).then_inc(setup, 1)
            layer_norm(1, link)
            normalised(1)
            split_rest(0, 0)
            split_last(0, 0)
            rounding_of_1p(0)
            make_dt(0, 0)
            make_u(0, 0)

            def step(i, first, last):
                for s in range(SLOTS):
                    half, n = s // N, s % N
                    c = 2 * i + half
                    k = i * SLOTS + s
                    scan(k, s)
                    if not (first and s == 0):
                        times_c(k - 1, (s - 1) % SLOTS)
                    if not (first and half == 0):
                        if n == 2:
                            skip(c - 1, 1 - half)
                        if n == 3:
                            gate(c - 1, 1 - half)
                        if n == 9:
                            residual(c - 1)
                    if not (last and half == 1):
                        if n == 9:
                            split_rest(c + 1, 1 - half)
                        if n == 11:
                            split_last(c + 1, 1 - half)
                        if n == 12:
                            rounding_of_1p(c + 1)
                        if n == 13:
                            make_dt(c + 1, 1 - half)
                            make_u(c + 1, 1 - half)
                    if not last:
                        if n == 10:
                            link = linker(v, Count(chain, (c + 2) * ln.LINKS))
                            layer_norm(c + 2, link)
                        if n == 14:
                            normalised(c + 2)
            two_groups(v, step)
            times_c(GROUPS * N - 1, SLOTS - 1)
            skip(GROUPS - 1, 1)
            gate(GROUPS - 1, 1)
            residual(GROUPS - 1)

        @block.scalar
        def _(act):
            act.preload_act_table_set(EXP_AND_LN)
            act.wait_ge(w_in, 16 * NW)
            act.activation(a_neg[:, :, :], a_neg[:, :, :], ACT.Exp).then_inc(a_exp, 1)
            act.wait_ge(setup, 1)
            act.wait_ge(consts, 3)

            def copy_xT(g):
                reach(act, z_psum, 2 * g)
                act.wait_ge(xT_psum, g + 1)
                act.activation(xnT[:, :, PAD:PAD + SEQ], pM[:, 0, :].rearrange("p (b t) -> p b t", t=SEQ),
                               ACT.Identity).then_inc(xnT_ready, 1)

            def copy_z(g, half):
                reach(act, zg_ready, g)
                act.wait_ge(z_psum, 2 * g + half + 1)
                act.activation(z[:, half, :], pM[:, 1 - half, :], ACT.Identity).then_inc(z_ready, 1)

            def silu_z(g):
                act.wait_ge(z_ready, 2 * g + 2)
                reach(act, y_ready, g)
                act.activation(z_gate[:, :, :], z[:, :, :], ACT.Silu).then_inc(zg_ready, 1)

            def silu_x(g, par):
                reach(act, y_used, g - 1)
                for half in range(2):
                    act.wait_ge(xs_psum, 2 * g + half + 1)
                    ins = act.activation(xs[:, par, half, :], pM[:, half, :], ACT.Silu, bias=conv_b[:, half:half + 1])
                ins.then_inc(xs_ready, 1)

            def split_first(g, par):
                act.wait_ge(xd_psum, g + 1)
                reach(act, c_psum, (g - 1) * N)
                act.activation(split[0:32, par, :], pM[0:32, 0, :], ACT.Identity).then_inc(hi_ready, 1)
                reach(act, dt_psum, 2 * g)
                act.activation(dt_low[:, :], pM[32:32 + RANK, 0, :], ACT.Identity).then_inc(low_ready, 1)

            def split_second(g, par):
                act.wait_ge(rest_ready, g + 1)
                act.activation(split[32:64, par, :], rest[32:64, :], ACT.Identity).then_inc(mid_ready, 1)

            def softplus(g):
                reach(act, dt_ready, g)
                act.wait_ge(dt_psum, 2 * g + 2)
                for half in range(2):
                    act.activation(absv[:, half, :], pM[:, 1 - half, :], ACT.Abs, bias=b_dt[:, half:half + 1])
                    ins = act.activation(relu[:, half, :], pM[:, 1 - half, :], ACT.Relu, bias=b_dt[:, half:half + 1])
                ins.then_inc(relu_ready, 1)
                act.wait_ge(relu_ready, g + 1)
                act.activation(e1[:, :, :], absv[:, :, :], ACT.Exp, scale=-1.0).then_inc(soft_link, 1)
                act.wait_ge(soft_link, 2 * g + 1)
                act.activation(e1p[:, :, :], e1[:, :, :], ACT.Identity, bias=1.0).then_inc(soft_link, 1)

            def logarithm(g):
                act.wait_ge(soft_link, 2 * g + 2)
                act.activation(lnv[:, :, :], e1p[:, :, :], ACT.Ln).then_inc(ln_ready, 1)

            def decay(k, s):
                reach(act, scan_done, k - 3)
                for half in range(2):
                    ins = act.activation(dA[:, s % 4, half, :, 1:SEQ],
                                         dt[:, s // N, half, :].rearrange("p (b t) -> p b t", t=SEQ)[:, :, 1:SEQ],
                                         ACT.Exp, scale=a_neg[:, half, s % N:s % N + 1])
                ins.then_inc(da_ready, 1)

            def copy_b(k, s):
                act.wait_ge(b_psum, k + 1)
                reach(act, dbx_ready, k - 3)
                act.activation(b_sb[:, s % 4, :], pB[:, s % 2, :], ACT.Identity).then_inc(b_ready, 1)

            copy_xT(0)
            silu_x(0, 0)
            act.preload_act_table_set(EXP_AND_LN)
            split_first(0, 0)
            split_second(0, 0)
            softplus(0)
            logarithm(0)

            def step(i, first, last):
                for s in range(SLOTS):
                    half, n = s // N, s % N
                    c = 2 * i + half
                    k = i * SLOTS + s
                    if n == 0:
                        act.wait_ge(dt_ready, c + 1)
                    decay(k, s)
                    copy_b(k, s)
                    if not (last and half == 1):
                        if n == 4:
                            copy_xT(c + 1)
                        if n == 11:
                            split_first(c + 1, 1 - half)
                        if n == 13:
                            split_second(c + 1, 1 - half)
                        if n == 14:
                            softplus(c + 1)
                            logarithm(c + 1)
                    if n == 1:
                        copy_z(c, 0)
                        copy_z(c, 1)
                    if n == 8:
                        silu_z(c)
                        if not (last and half == 1):
                            silu_x(c + 1, 1 - half)
                        act.preload_act_table_set(EXP_AND_LN)
            two_groups(act, step)

        @block.tensor
        def _(pe):
            pe.wait_ge(setup, 1)

            def turn_x(g):
                pe.wait_ge(xn_ready, g + 1)
                reach(pe, z_ready, 2 * g)
                for t in range(TILES):
                    ins = pe.transpose(pM[:, 0, t * P:(t + 1) * P], xn[:, t, :], ident[:, :])
                ins.then_inc(xT_psum, 1)

            def project_z(g, half):
                pe.wait_ge(relu_ready, g + 1)
                pe.matmul(pM[:, 1 - half, :].rearrange("p (b t) -> p b t", t=SEQ), w_in_t[:, 2 + half, :],
                          xnT[:, :, PAD:PAD + SEQ], start=True, stop=True).then_inc(z_psum, 1)

            def project_x(g, half, taps):
                if taps[0] == 0:
                    pe.wait_ge(xnT_ready, g + 1)
                for tap in taps:
                    ins = pe.matmul(pM[:, half, :].rearrange("p (b t) -> p b t", t=SEQ), w_taps[:, tap, half, :],
                                    xnT[:, :, tap:tap + SEQ], start=(tap == 0), stop=(tap == TAPS - 1))
                if taps[-1] == TAPS - 1:
                    ins.then_inc(xs_psum, 1)

            def project_bcdt(g, par):
                pe.wait_ge(xs_ready, g + 1)
                for half in range(2):
                    ins = pe.matmul(pM[0:XD, 0, :], w_x[:, half, :], xs[:, par, half, :], start=(half == 0),
                                    stop=(half == 1))
                ins.then_inc(xd_psum, 1)

            def project_dt(g):
                pe.wait_ge(low_ready, g + 1)
                reach(pe, o_done, g - 1)
                pe.matmul(pM[:, 1, :], w_dt[:, 0, :], dt_low[:, :], start=True, stop=True).then_inc(dt_psum, 1)
                pe.wait_ge(rest_ready, g + 1)
                pe.matmul(pM[:, 0, :], w_dt[:, 1, :], dt_low[:, :], start=True, stop=True).then_inc(dt_psum, 1)

            def send_b(k, s):
                reach(pe, b_ready, k - 1)
                pe.matmul(pB[:, s % 2, :], sel_bf[:, s % N, :], split[:, s // N, :], start=True,
                          stop=True).then_inc(b_psum, 1)

            def send_c(k, s):
                reach(pe, hc_ready, k - 1)
                pe.matmul(pC[:, s % 2, :], sel_bf[:, N + s % N, :], split[:, s // N, :], start=True,
                          stop=True).then_inc(c_psum, 1)

            def add_state(k, s, g):
                pe.wait_ge(hc_ready, k + 1)
                if s % N == 0:
                    reach(pe, y_used, g)
                for half in range(2):
                    ins = pe.matmul(pY[:, half, :], ident[:, :], hc[:, s % 4, half, :], start=(s % N == 0),
                                    stop=(s % N == N - 1))
                ins.then_inc(y_psum, 1)

            def project_out(g):
                pe.wait_ge(y_ready, g + 1)
                if isinstance(g, int) and g == GROUPS - 1:
                    pe.wait_ge(o_done, g)
                else:
                    pe.wait_ge(xs_ready, at_most(g + 3))
                    pe.wait_ge(z_ready, 2 * g + 4)
                for t in range(TILES):
                    for half in range(2):
                        ins = pe.matmul(pM[:, 1, t * P:(t + 1) * P], y_gated[:, half, t * P:(t + 1) * P],
                                        w_out_t[:, half, :], start=(half == 0), stop=(half == 1))
                ins.then_inc(o_psum, 1)

            turn_x(0)
            project_x(0, 0, range(TAPS))
            project_x(0, 1, range(TAPS))
            project_bcdt(0, 0)
            project_dt(0)
            pe.wait_ge(split_ready, 1)
            for k in range(AHEAD):
                send_b(k, k)
            project_z(0, 0)
            project_z(0, 1)

            def step(i, first, last):
                for s in range(SLOTS):
                    half, n = s // N, s % N
                    c = 2 * i + half
                    k = i * SLOTS + s
                    if n == N - AHEAD and not (last and half == 1):
                        pe.wait_ge(split_ready, c + 2)
                    if not (last and s >= SLOTS - AHEAD):
                        send_b(k + AHEAD, (s + AHEAD) % SLOTS)
                    if not (first and s < 1):
                        send_c(k - 1, (s - 1) % SLOTS)
                    if not (first and s < 3):
                        add_state(k - 3, (s - 3) % SLOTS, c if n >= 3 else c - 1)
                    if not (last and half == 1):
                        if n == 0:
                            turn_x(c + 1)
                        if n in (2, 3):
                            project_x(c + 1, 0, (0, 1) if n == 2 else (2, 3))
                        if n in (4, 5):
                            project_x(c + 1, 1, (0, 1) if n == 4 else (2, 3))
                        if n == 7:
                            project_bcdt(c + 1, 1 - half)
                        if n == 10:
                            project_dt(c + 1)
                        if n == 13:
                            project_z(c + 1, 0)
                            project_z(c + 1, 1)
                    if n == 8 and not (first and half == 0):
                        project_out(c - 1)
            two_groups(pe, step)
            K = GROUPS * N
            send_c(K - 1, SLOTS - 1)
            for k in range(K - 3, K):
                add_state(k, k % SLOTS, GROUPS - 1)
            project_out(GROUPS - 1)


class FfnWeights:

    DMAS = 4

    def __init__(self, nc, ctx, pre, w, gated):
        self.w, self.pre = w, pre
        self.hidden_chunks = 2 if gated else 4
        m = Memory(nc, ctx, pre + "w")
        ctx.callback(m.clear)
        self.w1 = m.sb("w1", [P, EXPERTS, 4, P])
        self.w2 = m.sb("w2", [P, EXPERTS, self.hidden_chunks, D])
        self.b1 = m.sb("b1", [P, EXPERTS, 4])
        self.b2 = m.sb("b2", [P, EXPERTS, D])
        self.loaded = m.sem("loaded")

    def load(self, sp):
        for buf, name in ((self.w1, "_w1"), (self.b1, "_b1"), (self.w2, "_w2")):
            sp.dma_start(everything(buf), self.w[self.pre + name]).then_inc(self.loaded, 16)
        sp.dma_start(self.b2[:, :, :], self.w[self.pre + "_b2"].partition_broadcast(P)).then_inc(self.loaded, 16)

    def wait(self, eng):
        eng.wait_ge(self.loaded, 16 * self.DMAS)


def ffn_phase(nc, pre, w, src, dst, gated, weights):
    HC = 2 if gated else 4
    MM = 4
    with ExitStack() as ctx:
        m = Memory(nc, ctx, pre)
        ctx.callback(m.clear)
        w1, w2, b1, b2 = weights.w1, weights.w2, weights.b1, weights.b2
        wr = m.sb("wr", [D, EXPERTS])
        ident = m.sb("ident", [P, P])
        rev = m.sb("rev", [P, EXPERTS])
        euler = m.sb("euler", [P, TILES * EXPERTS])
        xin = m.sb("xin", [P, TILES, D])
        ln = LayerNorm(m)
        xn = m.sb("xn", [P, TILES, D])
        xnT = m.sb("xnT", [D, GROUP])
        hT = m.sb("hT", [P, 2, HC, GROUP])
        sg = m.sb("sg", [P, 2, HC, GROUP]) if gated else None
        acc = m.sb("acc", [P, TILES, D])
        r8 = [m.sb(f"r8_{i}", [P, TILES, EXPERTS]) for i in range(8)]
        lgs, ex, key1, oh1, l2, key2, oh2, comb = r8
        r1 = [m.sb(f"r1_{i}", [P, TILES]) for i in range(7)]
        max1, kmax1, max2, kmax2, ssum, zsum, rsum = r1

        pT = m.ps("pT", [P, GROUP])
        plg = m.ps("plg", [P, GROUP])
        pH = m.ps("pH", [P, 4, GROUP])
        pY = m.ps("pY", [P, 2, TILES, D])

        weights_in = m.sem("weights_in")
        x_in = m.sem("x_in")
        x_out = m.sem("x_out")
        consts = m.sem("consts")
        var_ready = m.sem("var_ready")
        rstd_ready = m.sem("rstd_ready")
        xn_ready = m.sem("xn_ready")
        xT_psum = m.sem("xT_psum")
        xnT_ready = m.sem("xnT_ready")
        lg_ready = m.sem("lg_ready")
        lgs_ready = m.sem("lgs_ready")
        ex_ready = m.sem("ex_ready")
        comb_ready = m.sem("comb_ready")
        h_psum = m.sem("h_psum")
        act_done = m.sem("act_done")
        gated_done = m.sem("gated_done")
        y_psum = m.sem("y_psum")
        y_used = m.sem("y_used")
        acc_ready = m.sem("acc_ready")
        chain = m.sem("chain")

        block = ctx.enter_context(nc.Block())
        func = ACT.Silu if gated else ACT.Gelu_apprx_tanh
        NW = 3
        ACTS = HC if gated else MM
        LAST = GROUPS - 1
        E = EXPERTS

        def each_group(eng, step):
            step(0, True, False)
            with eng.Fori(1, LAST) as g:
                step(g, False, False)
            step(LAST, False, True)

        @block.sync
        def _(sp):
            sp.dma_start(xin[:, :, :], rows(src, 0)).then_inc(x_in, 16)
            for buf, name in ((ident, "ident"), (wr, pre + "_wr"), (rev, "rev")):
                sp.dma_start(everything(buf), w[name]).then_inc(weights_in, 16)

            def step(g, first, last):
                if not last:
                    sp.wait_ge(acc_ready, g * E + 1)
                    sp.dma_start(xin[:, :, :], rows(src, g + 1)).then_inc(x_in, 16)
                sp.wait_ge(acc_ready, g * E + E)
                sp.dma_start(rows(dst, g), acc[:, :, :]).then_inc(x_out, 16)
            each_group(sp, step)
            sp.wait_ge(x_out, 16 * GROUPS)

        @block.gpsimd
        def _(pool):
            pool.memset(euler[:, :], float(np.e)).then_inc(consts, 1)
            pool.memset(ln.minus_half[:, :], -0.5).then_inc(consts, 1)
            pool.wait_ge(consts, 2)
            pool.wait_ge(var_ready, 1)
            pool.tensor_tensor(ln.rstd[:, :], ln.var_eps[:, :], ln.minus_half[:, :], ALU.pow).then_inc(rstd_ready, 1)

            def step(g, first, last):
                pool.wait_ge(lgs_ready, g + 1)
                pool.tensor_tensor(ex[:, :, :].rearrange("p t e -> p (t e)"), euler[:, :],
                                   lgs[:, :, :].rearrange("p t e -> p (t e)"), ALU.pow).then_inc(ex_ready, 1)
                if not last:
                    pool.wait_ge(var_ready, g + 2)
                    pool.tensor_tensor(ln.rstd[:, :], ln.var_eps[:, :], ln.minus_half[:, :],
                                       ALU.pow).then_inc(rstd_ready, 1)
            each_group(pool, step)

        @block.vector
        def _(v):
            LN_LINKS = ln.LINKS
            PER_GROUP = LN_LINKS + (15 if gated else 14)
            def layer_norm(g, link):
                v.wait_ge(x_in, g * 16 + 16)
                layer_norm_stats(v, link, xin, ln)
                v.tensor_tensor(ln.var_eps[:, :], ln.m2[:, :], ln.dm2[:, :], ALU.add).then_inc(var_ready, 1)

            def normal(g):
                v.wait_ge(rstd_ready, g + 1)
                layer_norm_apply(v, xin, ln, xn).then_inc(xn_ready, 1)

            def logits_less_max(g, link):
                v.wait_ge(lg_ready, g + 1)
                lg = plg[:, 0:TILES * E].rearrange("p (t e) -> p t e", e=E)
                link(v.tensor_reduce(max1[:, :], lg, AX.X, ALU.max))
                v.tensor_tensor(lgs[:, :, :], lg, bc(max1[:, :], 2, E), ALU.subtract).then_inc(lgs_ready, 1)

            def router(g, link):
                v.wait_ge(lgs_ready, g + 1)
                revt = bc(rev[:, :], 1, TILES)
                link(v.scalar_tensor_tensor(key1[:, :, :], lgs[:, :, :], 0.0, revt, ALU.is_ge, ALU.mult))
                link(v.tensor_reduce(kmax1[:, :], key1[:, :, :], AX.X, ALU.max))
                link(v.tensor_tensor(oh1[:, :, :], key1[:, :, :], bc(kmax1[:, :], 2, E), ALU.is_equal))
                link(v.scalar_tensor_tensor(l2[:, :, :], oh1[:, :, :], -3e38, lgs[:, :, :], ALU.mult, ALU.add))
                link(v.tensor_reduce(max2[:, :], l2[:, :, :], AX.X, ALU.max))
                link(v.tensor_tensor(key2[:, :, :], l2[:, :, :], bc(max2[:, :], 2, E), ALU.is_equal))
                link(v.tensor_tensor(key2[:, :, :], key2[:, :, :], revt, ALU.mult))
                link(v.tensor_reduce(kmax2[:, :], key2[:, :, :], AX.X, ALU.max))
                link(v.tensor_tensor(oh2[:, :, :], key2[:, :, :], bc(kmax2[:, :], 2, E), ALU.is_equal))
                link(v.tensor_tensor(oh2[:, :, :], oh2[:, :, :], oh1[:, :, :], ALU.add))
                v.wait_ge(ex_ready, g + 1)
                link(v.tensor_tensor(comb[:, :, :], ex[:, :, :], oh2[:, :, :], ALU.mult))
                if gated:
                    v.tensor_reduce(zsum[:, :], ex[:, :, :], AX.X, ALU.add)
                link(v.tensor_reduce(ssum[:, :], comb[:, :, :], AX.X, ALU.add))
                if gated:
                    link(v.scalar_tensor_tensor(ssum[:, :], zsum[:, :], 1e-9, ssum[:, :], ALU.mult, ALU.add))
                link(v.reciprocal(rsum[:, :], ssum[:, :]))
                v.tensor_tensor(comb[:, :, :], comb[:, :, :], bc(rsum[:, :], 2, E), ALU.mult).then_inc(comb_ready, 1)
                v.wait_ge(comb_ready, g + 1)

            def gate_up(g, e):
                for c in range(HC):
                    v.wait_ge(act_done, g * (E * ACTS) + e * ACTS + c + 1)
                    v.wait_ge(h_psum, g * (E * MM) + e * MM + HC + c + 1)
                    v.scalar_tensor_tensor(hT[:, e % 2, c, :], pH[:, HC + c, :], b1[:, e, HC + c:HC + c + 1],
                                           sg[:, e % 2, c, :], ALU.add, ALU.mult).then_inc(gated_done, 1)

            def sum_expert(g, first, e, link):
                if e == 0 and not first:
                    v.wait_ge(x_out, g * 16)
                v.wait_ge(y_psum, g * E + e + 1)
                base = xin if e == 0 else acc
                for t in range(TILES):
                    ins = v.scalar_tensor_tensor(acc[:, t, :], pY[:, e % 2, t, :], comb[:, t, e:e + 1],
                                                 base[:, t, :], ALU.mult, ALU.add)
                ins.then_inc(y_used, 1)
                v.wait_ge(y_used, g * E + e + 1)
                for t in range(TILES):
                    ins = v.scalar_tensor_tensor(acc[:, t, :], b2[:, e, :], comb[:, t, e:e + 1],
                                                 acc[:, t, :], ALU.mult, ALU.add)
                ins.then_inc(acc_ready, 1)
                v.wait_ge(acc_ready, g * E + e + 1)

            count = Count(chain, 0)
            layer_norm(0, linker(v, count))
            normal(0)
            v.wait_ge(weights_in, 16 * NW)
            weights.wait(v)
            assert count.n == LN_LINKS

            def step(g, first, last):
                count = Count(chain, g * PER_GROUP + LN_LINKS)
                link = linker(v, count)
                logits_less_max(g, link)
                if gated:
                    gate_up(g, 0)
                    gate_up(g, 1)
                router(g, link)
                for e in range(E):
                    if gated and e > 0 and e + 1 < E:
                        gate_up(g, e + 1)
                    sum_expert(g, first, e, link)
                    if e == E - 5 and not last:
                        layer_norm(g + 1, link)
                    if e == E - 3 and not last:
                        normal(g + 1)
                assert last or count.n == PER_GROUP, count.n

            each_group(v, step)

        @block.scalar
        def _(act):
            weights.wait(act)

            def copy_xT(g):
                act.wait_ge(xT_psum, g + 1)
                act.activation(xnT[:, :], pT[:, :], ACT.Identity).then_inc(xnT_ready, 1)

            copy_xT(0)

            def step(g, first, last):
                for e in range(E):
                    for c in range(ACTS):
                        act.wait_ge(h_psum, g * (E * MM) + e * MM + c + 1)
                        if c == 0 and not (first and e < 2):
                            act.wait_ge(y_psum, g * E + e - 1)
                        out = sg if gated else hT
                        act.activation(out[:, e % 2, c, :], pH[:, c, :], func,
                                       bias=b1[:, e, c:c + 1]).then_inc(act_done, 1)
                if not last:
                    copy_xT(g + 1)
            each_group(act, step)

        @block.tensor
        def _(pe):
            pe.wait_ge(weights_in, 16 * NW)
            weights.wait(pe)

            def transposes(g):
                pe.wait_ge(xn_ready, g + 1)
                for t in range(TILES):
                    ins = pe.transpose(pT[:, t * P:(t + 1) * P], xn[:, t, :], ident[:, :])
                ins.then_inc(xT_psum, 1)

            def router(g):
                pe.wait_ge(xnT_ready, g + 1)
                for t in range(TILES):
                    ins = pe.matmul(plg[:, t * E:(t + 1) * E], xnT[:, t * P:(t + 1) * P], wr[:, :],
                                    start=True, stop=True)
                ins.then_inc(lg_ready, 1)

            def hidden(g, first, e):
                for c in range(MM):
                    if not (first and e == 0):
                        if c < ACTS:
                            pe.wait_ge(act_done, g * (E * ACTS) + (e - 1) * ACTS + c + 1)
                        else:
                            pe.wait_ge(gated_done, g * (E * HC) + (e - 1) * HC + c - HC + 1)
                    pe.matmul(pH[:, c, :], w1[:, e, c, :], xnT[:, :], start=True, stop=True).then_inc(h_psum, 1)

            def output(g, first, e):
                if gated:
                    pe.wait_ge(gated_done, g * (E * HC) + (e + 1) * HC)
                else:
                    pe.wait_ge(act_done, g * (E * ACTS) + (e + 1) * ACTS)
                if not (first and e < 2):
                    pe.wait_ge(y_used, g * E + e - 1)
                for t in range(TILES):
                    for c in range(HC):
                        ins = pe.matmul(pY[:, e % 2, t, :], hT[:, e % 2, c, t * P:(t + 1) * P], w2[:, e, c, :],
                                        start=(c == 0), stop=(c == HC - 1))
                ins.then_inc(y_psum, 1)

            transposes(0)

            def step(g, first, last):
                router(g)
                hidden(g, first, 0)
                for e in range(E):
                    if e + 1 < E:
                        hidden(g, first, e + 1)
                    elif not last:
                        transposes(g + 1)
                    output(g, first, e)
            each_group(pe, step)


def decoder_program(nc, w, y):
    between = [nc.dram_tensor(f"x_{i}", (TOKENS, D), F32).ap() for i in range(5)]
    mamba_phase(nc, "M", w, w["x"], between[0])
    with ExitStack() as ctx:
        weights = FfnWeights(nc, ctx, "F0", w, gated=False)
        attention_phase(nc, "X0", w, between[0], between[1], w["ctxT"], guarded=True, prefetch=weights)
        ffn_phase(nc, "F0", w, between[1], between[2], gated=False, weights=weights)
    attention_phase(nc, "S1", w, between[2], between[3], None, self_attn=True)
    with ExitStack() as ctx:
        weights = FfnWeights(nc, ctx, "F1", w, gated=True)
        attention_phase(nc, "X1", w, between[3], between[4], w["ctxT"], prefetch=weights)
        ffn_phase(nc, "F1", w, between[4], y, gated=True, weights=weights)


def layouts(i):
    f = {
        "x": i["x"].reshape(TOKENS, D),
        "ctxT": i["ctx_768"].reshape(TOKENS, DC).T,
        "ident": np.eye(P, dtype=np.float32),
        "mask": (np.arange(P)[:, None] // HD % 4 == np.arange(4)[None]).astype(np.float32),
        "quarter": (np.arange(P)[:, None] // 32 == np.arange(4)[None]).astype(np.float32),
        "rev": np.broadcast_to(np.arange(EXPERTS, 0, -1, dtype=np.float32), (P, EXPERTS)),
        "M_sel": (np.arange(96)[:, None] % 32 == np.arange(32)[None]).astype(np.float32),
    }
    n = "L0_attn_"
    f["M_w_in_t"] = i[n + "W_in"].T.reshape(D, 4, P)
    f["M_conv_w"] = i[n + "conv_w"].reshape(2, P, 4).transpose(2, 0, 1)
    f["M_conv_b"] = i[n + "conv_b"].reshape(2, P).T
    f["M_w_x"] = np.roll(i[n + "W_x"].T, -8, axis=1).reshape(2, P, 40).transpose(1, 0, 2)
    f["M_w_dt"] = i[n + "W_dt"].T.reshape(8, 2, P)
    f["M_b_dt"] = i[n + "b_dt"].reshape(2, P).T
    f["M_a_log"] = i[n + "A_log"].reshape(2, P, 16).transpose(1, 0, 2)
    f["M_d_skip"] = i[n + "D"].reshape(2, P).T
    f["M_w_out_t"] = i[n + "W_out"].T.reshape(2, P, D).transpose(1, 0, 2)

    def by_parity(a):
        return a.reshape(len(a), HEADS // 2, 2, HD).transpose(0, 2, 1, 3).reshape(len(a), 2, D // 2)

    for pre, n in (("X0", "L0_xattn_"), ("X1", "L1_xattn_")):
        f[pre + "_wq"], f[pre + "_wk"], f[pre + "_wo"] = i[n + "Wq"], i[n + "Wk"], i[n + "Wo"]
        f[pre + "_wv"], f[pre + "_bv"] = by_parity(i[n + "Wv"]), by_parity(i[n + "bv"][None])[0]
        f[pre + "_bq"], f[pre + "_bk"], f[pre + "_bo"] = i[n + "bq"][:, None], i[n + "bk"][:, None], i[n + "bo"]
    f["X0_wv_all"], f["X0_bv_col"] = i["L0_xattn_Wv"], i["L0_xattn_bv"][:, None]
    wt = i["L1_attn_in_proj_weight"].reshape(HEADS, 3, HD, D)
    bt = i["L1_attn_in_proj_bias"].reshape(HEADS, 3, HD)
    f["S1_wq"], f["S1_wk"] = (wt[:, k].reshape(P, D).T for k in range(2))
    f["S1_wv"] = by_parity(wt[:, 2].reshape(P, D).T)
    f["S1_wo"] = i["L1_attn_out_proj_weight"].T
    f["S1_bq"], f["S1_bk"] = (bt[:, k].reshape(P)[:, None] for k in range(2))
    f["S1_bv"], f["S1_bo"] = by_parity(bt[:, 2].reshape(1, P))[0], i["L1_attn_out_proj_bias"]

    f["F0_wr"], f["F0_b2"] = i["L0_ffn_Wg"], i["L0_ffn_b2"]
    f["F0_w1"] = i["L0_ffn_W1"].transpose(1, 0, 2).reshape(D, EXPERTS, 4, P)
    f["F0_w2"] = i["L0_ffn_W2"].reshape(EXPERTS, 4, P, D).transpose(2, 0, 1, 3)
    f["F0_b1"] = i["L0_ffn_b1"].reshape(EXPERTS, 4, P).transpose(2, 0, 1)
    n = "L1_ffn_"
    f["F1_wr"], f["F1_b2"] = i[n + "router_w"].T, i[n + "down_b"]
    f["F1_w1"] = np.concatenate([i[n + k].transpose(1, 0, 2).reshape(D, EXPERTS, 2, P) for k in ("gate_w", "up_w")], 2)
    f["F1_w2"] = i[n + "down_w"].reshape(EXPERTS, 2, P, D).transpose(2, 0, 1, 3)
    f["F1_b1"] = np.concatenate([i[n + k].reshape(EXPERTS, 2, P).transpose(2, 0, 1) for k in ("gate_b", "up_b")], 2)
    return {k: np.ascontiguousarray(a) for k, a in f.items()}


def kernel(**inputs):
    import concourse.bacc as _bacc
    from concourse.bass_utils import run_bass_kernel_spmd as _run

    nc = _bacc.Bacc("TRN2", target_bir_lowering=False, num_devices=1)
    arrays, w = {}, {}
    for name, a in layouts({k: np.asarray(a) for k, a in inputs.items()}).items():
        arrays[f"in_{name}"] = a
        w[name] = nc.dram_tensor(f"in_{name}", a.shape, mybir.dt.from_np(a.dtype), kind="ExternalInput").ap()
    y = nc.dram_tensor("out", (TOKENS, D), F32, kind="ExternalOutput").ap()
    decoder_program(nc, w, y)
    r = _run(nc, [arrays], core_ids=[0])
    return r.results[0]["out"].reshape(BATCH, SEQ, D)
```
